# Optimizing a Trainium2 kernel written in Bass

```python
import numpy as np
import jax
import jax.numpy as jnp

def _softmax(x, axis=-1):
    return jax.nn.softmax(x, axis=axis)

def _gelu(x):
    return jax.nn.gelu(x, approximate=True)

def _silu(x):
    return jax.nn.silu(x)

def _sigmoid(x):
    return jax.nn.sigmoid(x)

def _layernorm(x, axis=-1, eps=1e-05):
    m = jnp.mean(x, axis=axis, keepdims=True)
    v = jnp.var(x, axis=axis, keepdims=True)
    return (x - m) / jnp.sqrt(v + eps)

def _scatter_add(tgt, idx, src, axis=0):
    return tgt.at[idx].add(src)

def _segment_sum(src, seg, n):
    return jax.ops.segment_sum(src, seg, n)
kernel_name = 'mk_adj_preln_d2_adj_r2_9d2d4d'

def setup_inputs(seed: int=0):
    np.random.seed(seed)
    _w = jnp.asarray

    def _rec_inputs():
        import jax
        import jax.numpy as jnp
        _gk = jax.random.key(seed)
        x = -0.000929 + 1 * jax.random.normal(jax.random.fold_in(_gk, 1), (8192, 128), jnp.float32)
        _w = (1.0 + jnp.arange(8192, dtype=jnp.float32)) ** (-0.5)
        _w = _w / _w.mean()
        _pij = jnp.clip(0.00195312 * _w[:, None] * _w[None, :], 0.0, 1.0)
        _a = jax.random.uniform(jax.random.fold_in(_gk, 2), (8192, 8192)) < _pij
        _a = jnp.logical_or(_a, jnp.eye(8192, dtype=bool))
        _af = _a.astype(jnp.float32)
        _af = _af * jax.random.uniform(jax.random.fold_in(_gk, 3), (8192, 8192), jnp.float32, 0.05, 1)
        adj = _af
        return (x, adj)
    x, adj = _rec_inputs()

    def _L0_gnn_setup():
        import jax, jax.numpy as jnp
        import numpy as np
        N = 4096
        D_IN = 128
        D_OUT = 128
        key = jax.random.key(seed)
        k1, k2, k3, k4 = jax.random.split(key, 4)
        x = jax.random.normal(k1, (N, D_IN), dtype=jnp.float32)
        adj = jax.random.uniform(k2, (N, N), dtype=jnp.float32)
        bound = 1.0 / np.sqrt(D_IN)
        W = jax.random.uniform(k3, (D_OUT, D_IN), minval=-bound, maxval=bound, dtype=jnp.float32)
        b = jax.random.uniform(k4, (D_OUT,), minval=-bound, maxval=bound, dtype=jnp.float32)
        return {'x': x, 'adj': adj, 'W': W, 'b': b}
    _L0_gnn_all = _L0_gnn_setup()
    _L0_gnn_in = {k: v for k, v in _L0_gnn_all.items() if k in ('W', 'b')}
    del _L0_gnn_all

    def _L1_gnn_setup():
        import jax, jax.numpy as jnp
        import numpy as np
        MIN_NORM = 1e-15
        PROJ_EPS = 1e-05
        C = 1.0

        def artanh(x):
            x = jnp.clip(x, -1.0 + 1e-07, 1.0 - 1e-07)
            return 0.5 * (jnp.log1p(x) - jnp.log1p(-x))

        def logmap0(p, c):
            sqrt_c = c ** 0.5
            norm = jnp.maximum(jnp.linalg.norm(p, axis=-1, keepdims=True), MIN_NORM)
            return p * (artanh(sqrt_c * norm) / (sqrt_c * norm))

        def expmap0(u, c):
            sqrt_c = c ** 0.5
            norm = jnp.maximum(jnp.linalg.norm(u, axis=-1, keepdims=True), MIN_NORM)
            return jnp.tanh(sqrt_c * norm) * u / (sqrt_c * norm)

        def proj(x, c):
            norm = jnp.maximum(jnp.linalg.norm(x, axis=-1, keepdims=True), MIN_NORM)
            maxnorm = (1.0 - PROJ_EPS) / c ** 0.5
            return jnp.where(norm > maxnorm, x / norm * maxnorm, x)

        def dense_att(x, adj, w, b):
            d = x.shape[-1]
            s_left = x @ w[:d]
            s_right = x @ w[d:]
            score = jax.nn.sigmoid(s_left[:, None] + s_right[None, :] + b[0])
            return adj * score
        key = jax.random.key(seed)
        k1, k2, k3, k4 = jax.random.split(key, 4)
        n, d = (4096, 128)
        x = jax.random.normal(k1, (n, d), jnp.float32) * 0.01
        adj = (jax.random.uniform(k2, (n, n), jnp.float32) < 0.005).astype(jnp.float32)
        std = 1.0 / np.sqrt(2 * d)
        w_par = jax.random.normal(k3, (2 * d,), jnp.float32) * std
        w_chi = jax.random.normal(k4, (2 * d,), jnp.float32) * std
        b_par = jnp.zeros((1,), jnp.float32)
        b_chi = jnp.zeros((1,), jnp.float32)
        return {'x': x, 'adj': adj, 'w_par': w_par, 'b_par': b_par, 'w_chi': w_chi, 'b_chi': b_chi}
    _L1_gnn_all = _L1_gnn_setup()
    _L1_gnn_in = {k: v for k, v in _L1_gnn_all.items() if k in ('w_par', 'b_par', 'w_chi', 'b_chi')}
    del _L1_gnn_all
    return {'x': x, 'adj': adj, 'L0_gnn_W': _L0_gnn_in['W'], 'L0_gnn_b': _L0_gnn_in['b'], 'L1_gnn_w_par': _L1_gnn_in['w_par'], 'L1_gnn_b_par': _L1_gnn_in['b_par'], 'L1_gnn_w_chi': _L1_gnn_in['w_chi'], 'L1_gnn_b_chi': _L1_gnn_in['b_chi']}

def reference(x, adj, L0_gnn_W, L0_gnn_b, L1_gnn_w_par, L1_gnn_b_par, L1_gnn_w_chi, L1_gnn_b_chi):
    import jax
    import jax.numpy as jnp

    def _L0_gnn_ref(x, adj, W, b):
        import jax, jax.numpy as jnp
        import numpy as np
        N = 4096
        D_IN = 128
        D_OUT = 128
        rowsum = adj.sum(axis=1)
        d_inv_sqrt = jnp.power(rowsum, -0.5)
        d_inv_sqrt = jnp.where(jnp.isinf(d_inv_sqrt), 0.0, d_inv_sqrt)
        adj_norm = d_inv_sqrt[:, None] * adj * d_inv_sqrt[None, :]
        h = adj_norm @ x
        return h @ W.T + b

    def _L1_gnn_ref(x, adj, w_par, b_par, w_chi, b_chi):
        import jax, jax.numpy as jnp
        import numpy as np
        MIN_NORM = 1e-15
        PROJ_EPS = 1e-05
        C = 1.0

        def artanh(x):
            x = jnp.clip(x, -1.0 + 1e-07, 1.0 - 1e-07)
            return 0.5 * (jnp.log1p(x) - jnp.log1p(-x))

        def logmap0(p, c):
            sqrt_c = c ** 0.5
            norm = jnp.maximum(jnp.linalg.norm(p, axis=-1, keepdims=True), MIN_NORM)
            return p * (artanh(sqrt_c * norm) / (sqrt_c * norm))

        def expmap0(u, c):
            sqrt_c = c ** 0.5
            norm = jnp.maximum(jnp.linalg.norm(u, axis=-1, keepdims=True), MIN_NORM)
            return jnp.tanh(sqrt_c * norm) * u / (sqrt_c * norm)

        def proj(x, c):
            norm = jnp.maximum(jnp.linalg.norm(x, axis=-1, keepdims=True), MIN_NORM)
            maxnorm = (1.0 - PROJ_EPS) / c ** 0.5
            return jnp.where(norm > maxnorm, x / norm * maxnorm, x)

        def dense_att(x, adj, w, b):
            d = x.shape[-1]
            s_left = x @ w[:d]
            s_right = x @ w[d:]
            score = jax.nn.sigmoid(s_left[:, None] + s_right[None, :] + b[0])
            return adj * score
        x_tangent = logmap0(x, C)
        adj_att_par = dense_att(x_tangent, adj, w_par, b_par)
        adj_att_chi = dense_att(x_tangent, adj.T, w_chi, b_chi)
        support_t = adj_att_chi @ x_tangent + adj_att_par @ x_tangent
        return proj(expmap0(support_t, C), C)
    h = jnp.maximum(_layernorm(x, axis=-1), 0.0)
    x = x + _L0_gnn_ref(h, adj, L0_gnn_W, L0_gnn_b)
    h = jnp.maximum(_layernorm(x, axis=-1), 0.0)
    x = x + _L1_gnn_ref(h, adj, L1_gnn_w_par, L1_gnn_b_par, L1_gnn_w_chi, L1_gnn_b_chi)
    return x

_drawn_inputs = setup_inputs


def setup_inputs(seed=0):
    import zlib

    import numpy as np

    out = dict(_drawn_inputs(seed))
    spreads = {}
    factors = {'L1_gnn_w_par': 24.931, 'L1_gnn_w_chi': 28.932}
    for name, (base, spread) in spreads.items():
        noise = np.random.default_rng([zlib.crc32(name.encode()), seed]).standard_normal(out[name].shape)
        drawn = base * np.exp(spread * noise) if base else spread * noise
        out[name] = jnp.asarray(drawn.astype(out[name].dtype))
    for name, factor in factors.items():
        out[name] = (out[name] * factor).astype(out[name].dtype)
    return out
```

```python
import concourse.bass as bass
from concourse import mybir
from contextlib import ExitStack

F32 = mybir.dt.float32
U32 = mybir.dt.uint32
BF16 = mybir.dt.bfloat16
ALU = mybir.AluOpType
ACT = mybir.ActivationFunctionType
AX = mybir.AxisListType.X

P = 128
KT = 4
B = P * KT
LN_EPS = 1e-5
ARTANH_MAX = 1.0 - 1e-7
MIN_NORM_SQ = 1e-30
MAX_NORM = 1.0 - 1e-5
SERIES_SQ = 0.0625
RSQRT_SEED = 0x5F3759DF


class Segment:

    def __init__(self, n, j0, bs, blocks, a_use, products, y_use):
        self.n, self.j0, self.bs = n, j0, bs
        self.blocks = blocks
        self.a_use, self.products, self.y_use = dict(a_use), dict(products), dict(y_use)


class Panel:

    def __init__(self, phase, G, index):
        self.phase, self.G, self.index = phase, G, index
        self.segments = []
        self.products_before = {}


def plan_panels(NB):
    panels = []
    blocks = 0
    products = dict.fromkeys(range(4), 0)
    y_use = dict.fromkeys(range(2), 0)
    for phase in (1, 2):
        for G in range(NB):
            q, e = divmod(G, 4)
            pan = Panel(phase, G, len([x for x in panels if x.phase == 2 or x.G > 0]))
            pan.products_before = dict(products)
            if phase == 1:
                todo = [(q, 0, range(4)), (1, q, range(e))]
            else:
                todo = [(1, q, range(e, 4)), (3 - q, q + 1, range(4))]
            for n, j0, bs in todo:
                bs = list(bs)
                if not n or not bs:
                    continue
                if phase == 1:
                    a_use = {b: 4 * G + j0 for b in range(4)}
                else:
                    a_use = {b: NB * 4 + products[b] - first_pass[b] for b in range(4)}
                pan.segments.append(Segment(n, j0, bs, blocks, a_use, products, y_use))
                blocks += n * len(bs)
                for b in bs:
                    products[b] += n
                    y_use[b % 2] += n
            panels.append(pan)
        if phase == 1:
            first_pass = dict(products)
    return panels, products, y_use, blocks


def gnn_kernel(nc, x, adj, W0, b0, w_par, b_par, w_chi, b_chi, out, x1_dram, t_dram):
    N, D = x.shape
    NB = N // B
    NT = N // P
    assert D == P and NB == 16

    adj_v = adj.rearrange("(g m p) (h c) -> g h p m c", m=KT, p=P, c=B)
    x_v = x.rearrange("(g m p) d -> g p m d", m=KT, p=P)
    out_v = out.rearrange("(g m p) d -> g p m d", m=KT, p=P)
    x1_v = x1_dram.rearrange("(g m p) d -> g p m d", m=KT, p=P)
    t_v = t_dram.rearrange("(g m p) d -> g p m d", m=KT, p=P)

    panels, products_all, y_use_all, blocks_all = plan_panels(NB)
    pass1 = [p for p in panels if p.phase == 1]
    pass2 = [p for p in panels if p.phase == 2]
    products_pass1 = pass2[0].products_before

    ctx = ExitStack()
    with ctx:
        def sb(name, shape, dt=F32):
            return ctx.enter_context(nc.sbuf_tensor(name, shape, dt))

        def sem(name):
            return ctx.enter_context(nc.semaphore(name))

        left_par_bc = sb("left_par_bc", [P, N])
        left_chi_bc = sb("left_chi_bc", [P, N])
        outT = sb("outT", [P, N])
        ablk = sb("ablk", [P, 4, KT, B])
        shared = sb("shared", [P, N])
        temps = sb("temps", [P, N + B])
        right = sb("right", [P, NT, 2])
        dinv = sb("dinv", [P, NT])
        rowparts = sb("rowparts", [P, KT, NB])
        ident = sb("ident", [P, P])
        W_sb = sb("W_sb", [P, P])
        WT = sb("WT", [P, P])
        b_bc = sb("b_bc", [P, P])
        w_left = sb("w_left", [P, 2])
        w_right = sb("w_right", [P, 2])
        w_left_rep = sb("w_left_rep", [P, 2, P])
        bias2 = sb("bias2", [P, 2])
        zeros_bf = sb("zeros_bf", [P, B], BF16)
        small = sb("small", [P, 24, 2 * KT])
        fin = sb("fin", [P, 8, NT])

        y_sb = shared[:, :].rearrange("p (g c) -> p g c", c=B)
        at = temps[:, 0:4 * B].rearrange("p (r k c) -> p r k c", r=2, k=2)
        y_slot = temps[:, 4 * B:6 * B].rearrange("p (r c) -> p r c", r=2)
        x_buf = temps[:, 6 * B:8 * B].rearrange("p (r c) -> p r c", r=2)
        cen_buf = temps[:, 8 * B:10 * B].rearrange("p (r c) -> p r c", r=2)
        sq_buf = temps[:, 10 * B:12 * B].rearrange("p (r c) -> p r c", r=2)
        x1_buf = temps[:, 12 * B:14 * B].rearrange("p (r c) -> p r c", r=2)
        t_buf = temps[:, 14 * B:16 * B].rearrange("p (r c) -> p r c", r=2)
        tT = temps[:, 16 * B:17 * B]
        h_buf = cen_buf[:, 0, :]
        hsq_buf = cen_buf[:, 1, :]
        z_buf = sq_buf
        x1_all = temps[:, 0:N].rearrange("p (g c) -> p g c", c=B)
        sig_par = shared[:, 0:4 * B].rearrange("p (r k c) -> p r k c", r=2, k=2)
        chi = shared[:, 4 * B:10 * B].rearrange("p (r k c) -> p r k c", r=3, k=2)
        mix = shared[:, 10 * B:14 * B].rearrange("p (r k c) -> p r k c", r=2, k=2)
        tg = [shared[:, 14 * B:16 * B].rearrange("p (k c) -> p k c", k=2), sb("tg1", [P, 2, B])[:, :, :]]
        s_all = ablk[:, :, :, :].rearrange("p a m c -> p (a m) c")

        T = ctx.enter_context(nc.psum_tensor("T", [P, 2, 2, B], F32))
        acc = [ctx.enter_context(nc.psum_tensor(f"acc{i}", [P, B], F32)) for i in range(2)]
        U = ctx.enter_context(nc.psum_tensor("U", [P, B], F32))

        a_loaded = [sem(f"a_loaded{s}") for s in range(4)]
        rowsummed = [sem(f"rowsummed{s}") for s in range(4)]
        transposed = [sem(f"transposed{s}") for s in range(4)]
        half_ready = sem("half_ready")
        half_free = sem("half_free")
        at_used = sem("at_used")
        y_copied = [sem(f"y_copied{s}") for s in range(2)]
        x_loaded = [sem(f"x_loaded{s}") for s in range(2)]
        mean_ready = sem("mean_ready")
        centred = sem("centred")
        y_done = sem("y_done")
        acc_done = sem("acc_done")
        acc_stored = sem("acc_stored")
        const_loaded = sem("const_loaded")
        const_ready = sem("const_ready")
        wt_psum = sem("wt_psum")
        wt_ready = sem("wt_ready")
        zero_ready = sem("zero_ready")
        reps_ready = sem("reps_ready")
        z_done = sem("z_done")
        u_done = sem("u_done")
        u_read = sem("u_read")
        xb_ready = sem("xb_ready")
        x1_ready = sem("x1_ready")
        ln_in = sem("ln_in")
        ln_out = sem("ln_out")
        t_ready = sem("t_ready")
        tT_done = sem("tT_done")
        outT_zeroed = sem("outT_zeroed")
        x1_stored = [sem(f"x1_stored{s}") for s in range(2)]
        t_stored = [sem(f"t_stored{s}") for s in range(2)]
        layer0_over = sem("layer0_over")
        dve_step = sem("dve_step")
        act_turns = sem("act_turns")
        sp_turns = sem("sp_turns")
        pool_step = sem("pool_step")
        pool_steps = [0]
        pair_loaded = [sem(f"pair_loaded{s}") for s in range(2)]
        turned = sem("turned")
        par_sig = sem("par_sig")
        chi_sig = sem("chi_sig")
        chi_done = sem("chi_done")
        par_done = sem("par_done")
        mixed = sem("mixed")
        unit_used = sem("unit_used")
        outh_added = sem("outh_added")
        outg_added = sem("outg_added")
        x1_back = sem("x1_back")
        s_turned = sem("s_turned")
        s_copied = sem("s_copied")
        s_squared = sem("s_squared")
        norm_in = sem("norm_in")
        tanh_out = sem("tanh_out")
        fin_ready = sem("fin_ready")
        out_stored = sem("out_stored")

        block = ctx.enter_context(nc.Block())

        USES0 = {s: 4 * NB + products_all[s] - products_pass1[s] for s in range(4)}
        HALVES0 = 2 * blocks_all
        SV_HALVES = 4

        def halves_before(pan, seg):
            extra = 0
            if pan.phase == 2:
                done = max(pan.G - 2, 0)
                if seg is not pan.segments[0] and pan.G >= 2:
                    done += 1
                extra = SV_HALVES * done
            return 2 * seg.blocks + extra

        def sv_halves_before(g):
            if g <= NB - 3:
                pan = pass2[g + 2]
                first = pan.segments[0]
                return 2 * (first.blocks + first.n * len(first.bs)) + SV_HALVES * g
            return HALVES0 + SV_HALVES * g

        def each_run(eng, seg, body):
            if seg.n > 1:
                with eng.Fori(0, seg.n) as j:
                    body(j)
            else:
                body(0)

        def positions(G):
            for i in range(NB // 2):
                yield i, i % 2, G * (NB // 4) + i // 2, G * 30 + (4 * i - 2 if i else 0)

        UNITS_G = 30
        TAIL_UNIT = UNITS_G * NB
        TAIL_USE = NB * (NB // 4)

        @block.sync
        def _(sp):
            sp.dma_start(x_buf[:, 0, :].rearrange("p (m d) -> p m d", m=KT), x_v[0]).then_inc(x_loaded[0], 16)
            for pan in pass1:
                G = pan.G
                q, e = divmod(G, 4)
                if G + 1 < NB:
                    s = (G + 1) % 2
                    if G >= 1:
                        sp.wait_ge(centred, G)
                    sp.dma_start(x_buf[:, s, :].rearrange("p (m d) -> p m d", m=KT), x_v[G + 1]).then_inc(x_loaded[s], 16)

                def load(j, H, s, products):
                    sp.wait_ge(rowsummed[s], 4 * G + 1 + j)
                    sp.sem_inc(sp_turns, 1)
                    sp.wait_ge(transposed[s], products)
                    sp.dma_start(ablk[:, s, :, :], adj_v[G, H]).then_inc(a_loaded[s], 16)

                before = pan.products_before
                if q > 1:
                    with sp.Fori(0, q) as j:
                        for s in range(4):
                            load(j, 4 * j + s, s, before[s] + j + 1)
                elif q == 1:
                    for s in range(4):
                        load(0, s, s, before[s] + 1)
                for s in range(4):
                    load(q, 4 * q + s, s, before[s] + q + 1)
                for jj in range(q + 1, 4):
                    for s in range(4):
                        load(jj, 4 * jj + s, s, before[s] + q + (s < e) + 1)
            for pan in pass2:
                G = pan.G
                s = G % 2
                if G >= 2:
                    sp.wait_ge(x1_ready, G - 1)
                else:
                    sp.wait_ge(centred, NB)
                sp.dma_start(x_buf[:, s, :].rearrange("p (m d) -> p m d", m=KT), x_v[G]).then_inc(x_loaded[s], 16)
                for seg in pan.segments:
                    def run(j):
                        for b in seg.bs:
                            sp.wait_ge(rowsummed[b], 4 * NB + 1)
                            sp.wait_ge(transposed[b], seg.products[b] + 1 + j)
                            sp.dma_start(ablk[:, b, :, :], adj_v[G, 4 * (seg.j0 + j) + b]).then_inc(a_loaded[b], 16)
                    each_run(sp, seg, run)

            sp.wait_ge(layer0_over, 4)
            for s in range(2):
                sp.wait_ge(t_stored[s], 16 * NB // 2)
                sp.wait_ge(x1_stored[s], 16 * NB // 2)

            def tile_of(a):
                return a.rearrange("p (m d) -> p m d", m=KT)

            def load_pair(G, H, slot, last_unit):
                sp.wait_ge(unit_used, last_unit + 6)
                sp.wait_ge(chi_done, last_unit + 6)
                if H is None:
                    sp.dma_start(ablk[:, 2 * slot + 1, :, :], adj_v[G, G]).then_inc(pair_loaded[slot], 32)
                    sp.dma_start(tile_of(tg[slot][:, 0, :]), t_v[G]).then_inc(pair_loaded[slot], 32)
                else:
                    sp.dma_start(ablk[:, 2 * slot + 1, :, :], adj_v[H, G]).then_inc(pair_loaded[slot], 16)
                    sp.dma_start(ablk[:, 2 * slot, :, :], adj_v[G, H]).then_inc(pair_loaded[slot], 16)
                    sp.dma_start(tile_of(tg[slot][:, 0, :]), t_v[G]).then_inc(pair_loaded[slot], 16)
                    sp.dma_start(tile_of(tg[slot][:, 1, :]), t_v[H]).then_inc(pair_loaded[slot], 16)

            with sp.Fori(0, NB) as G:
                for r, slot, _, unit in positions(G):
                    load_pair(G, (G + r) % NB if r else None, slot, unit - (5, 3, 5)[min(r, 2)])
            for g in range(NB // 2):
                load_pair(g, g + NB // 2, g % 2, TAIL_UNIT + 4 * g - 5)
            for g in range(NB):
                sp.dma_start(tile_of(x1_all[:, g, :]), x1_v[g]).then_inc(x1_back, 16)
            for g in range(NB):
                sp.wait_ge(fin_ready, g + 1)
                sp.dma_start(out_v[g], tile_of(s_all[:, g, :])).then_inc(out_stored, 16)
            sp.wait_ge(out_stored, 16 * NB)

        @block.tensor
        def _(pe):
            for s in range(4):
                pe.sem_inc(transposed[s], 1)
            pe.sem_inc(at_used, 3)
            pe.sem_inc(unit_used, 5)
            pe.wait_ge(const_loaded, 16 * 8)
            pe.wait_ge(const_ready, 1)
            nc.tensor.transpose(U[:, 0:P], W_sb[:, :], ident[:, :]).then_inc(wt_psum, 1)
            pe.wait_ge(reps_ready, 2)

            def u_part(g):
                pe.wait_ge(z_done, g + 1)
                if g == 0:
                    pe.wait_ge(wt_ready, 1)
                else:
                    pe.wait_ge(u_read, g)
                for k in range(KT):
                    mm = nc.tensor.matmul(U[:, k * P:(k + 1) * P], z_buf[:, g % 2, k * P:(k + 1) * P], WT[:, :],
                                          start=True, stop=True)
                mm.then_inc(u_done, 1)

            def score_vectors(g):
                h = sv_halves_before(g)
                pe.wait_ge(t_ready, g + 1)
                pe.wait_ge(half_free, h + 1)
                for k in range(KT):
                    mm = nc.tensor.transpose(T[:, 0, 0, k * P:(k + 1) * P], t_buf[:, g % 2, k * P:(k + 1) * P], ident[:, :])
                mm.then_inc(half_ready, 1)
                pe.wait_ge(half_free, h + 3)
                nc.tensor.matmul(T[:, 1, 0, :], w_left_rep[:, 0, :], tT, start=True, stop=True).then_inc(half_ready, 1)
                nc.tensor.matmul(T[:, 0, 0, :], w_left_rep[:, 1, :], tT, start=True, stop=True).then_inc(half_ready, 1)
                pe.wait_ge(half_free, h + 4)
                for k in range(KT):
                    mm = nc.tensor.matmul(T[:, 1, 0, 2 * k:2 * k + 2], tT[:, k * P:(k + 1) * P], w_right[:, :],
                                          start=True, stop=True)
                mm.then_inc(half_ready, 1)
                pe.wait_ge(half_free, h + 6)
                pe.sem_inc(at_used, SV_HALVES)

            for pan in panels:
                if not pan.segments:
                    continue
                G, i = pan.G, pan.index
                bank = acc[i % 2]
                if i >= 2:
                    if i - 2 < NB - 1:
                        pe.wait_ge(acc_stored, i - 1)
                    else:
                        pe.wait_ge(z_done, i - 2 - (NB - 1) + 1)
                nc.tensor.matmul(bank[:, :], zeros_bf[:, 0:P], zeros_bf[:, :], start=True, stop=False)
                for seg in pan.segments:
                    h0 = halves_before(pan, seg)
                    nb = len(seg.bs)

                    def run(j):
                        def turn(i2):
                            n, half = divmod(i2, 2)
                            b = seg.bs[n]
                            if half == 0:
                                pe.wait_ge(a_loaded[b], 16 * (seg.a_use[b] + 1) + 16 * j)
                            pe.wait_ge(half_free, h0 + i2 + 1 + 2 * nb * j)
                            for k in range(2):
                                for m in range(KT):
                                    c = (2 * half + k) * P
                                    mm = nc.tensor.transpose(T[:, half, k, m * P:(m + 1) * P],
                                                             ablk[:, b, m, c:c + P], ident[:, :])
                            mm.then_inc(half_ready, 1)

                        def multiply(i2, turned_block):
                            n, half = divmod(i2, 2)
                            ys = (seg.blocks + n) % 2
                            if half == 0:
                                pe.wait_ge(y_copied[ys], (seg.blocks + n) // 2 + 1 + nb // 2 * j)
                            pe.wait_ge(half_free, h0 + i2 + 3 + 2 * nb * j)
                            for k in range(2):
                                c = (2 * half + k) * P
                                mm = nc.tensor.matmul(bank[:, :], y_slot[:, ys, c:c + P], at[:, half, k, :],
                                                      start=False, stop=False)
                                if k == 0 and turned_block is not None:
                                    mm.then_inc(transposed[turned_block], 1)
                            mm.then_inc(at_used, 1)

                        turn(0)
                        for i2 in range(1, 2 * nb):
                            turn(i2)
                            multiply(i2 - 1, seg.bs[i2 // 2] if i2 % 2 else None)
                        multiply(2 * nb - 1, None)

                    each_run(pe, seg, run)
                    if pan.phase == 2 and seg is pan.segments[0]:
                        if G >= 1:
                            u_part(G - 1)
                        if G >= 2:
                            score_vectors(G - 2)
                nc.tensor.matmul(bank[:, :], zeros_bf[:, 0:P], zeros_bf[:, :], start=False, stop=True).then_inc(acc_done, 1)
            u_part(NB - 1)
            score_vectors(NB - 2)
            score_vectors(NB - 1)
            pe.drain().then_inc(layer0_over, 1)
            pe.wait_ge(layer0_over, 4)

            outg, outh = acc[0], acc[1]

            def turn(d, slot, blk, half, unit, first_of_use=None):
                if first_of_use is not None:
                    pe.wait_ge(pair_loaded[slot], 64 * first_of_use + 64)
                pe.wait_ge(mixed, unit + 2)
                for k in range(2):
                    for m in range(KT):
                        c = (2 * half + k) * P
                        mm = nc.tensor.transpose(T[:, d % 2, k, m * P:(m + 1) * P], ablk[:, 2 * slot + blk, m, c:c + P],
                                                 ident[:, :])
                mm.then_inc(turned, 1)

            def multiply(d, slot, which, half, unit, bank, start, stop):
                pe.wait_ge(mixed, unit + 4)
                for k in range(2):
                    c = (2 * half + k) * P
                    mm = nc.tensor.matmul(bank[:, :], tg[slot][:, which, c:c + P], mix[:, d % 2, k, :],
                                          start=start and k == 0, stop=stop and k == 1)
                mm.then_inc(unit_used, 1)

            def units_of(i, slot, use, unit0, tail):
                if i == 0 and not tail:
                    for half in range(2):
                        yield half, slot, 1, half, use if half == 0 else None, 0, outg, unit0 + half
                else:
                    for v in range(4):
                        o_is_g = v >= 2
                        yield (4 * i - 2 + v, slot, 0 if o_is_g else 1, v % 2, use if v == 0 else None,
                               1 if o_is_g else 0, outg if o_is_g else outh, unit0 + v)

            def stream(units, nxt, starts, stops, before):
                for n, (d, slot, blk, half, fu, which, bank, unit) in enumerate(units):
                    if n + 1 < len(units):
                        d2, s2, blk2, half2, fu2, _, _, unit2 = units[n + 1]
                        turn(d2, s2, blk2, half2, unit2, fu2)
                    elif nxt:
                        nxt()
                    before(n)
                    multiply(d, slot, which, half, unit, bank, starts(n), stops(n))

            turn(0, 0, 1, 0, 0, 0)
            with pe.Fori(0, NB) as G:
                units = [u for i, slot, use, unit0 in positions(G) for u in units_of(i, slot, use, unit0, False)]

                def before(n):
                    if n == 0:
                        pe.wait_ge(outg_added, G + 1)
                    elif n >= 2 and (n - 2) % 4 == 0:
                        pe.wait_ge(outh_added, 7 * G + (n - 2) // 4 + 1)

                stream(units, lambda: turn(0, 0, 1, 0, UNITS_G * G + UNITS_G, (NB // 4) * G + NB // 4),
                       lambda n: n == 0 or (n >= 2 and (n - 2) % 4 == 0),
                       lambda n: n == UNITS_G - 1 or (n >= 2 and (n - 2) % 4 == 1), before)
            tail = [u for g in range(NB // 2)
                    for u in units_of(0, g % 2, TAIL_USE + g // 2, TAIL_UNIT + 4 * g, True)]
            tail = [(n % 2, *u[1:]) for n, u in enumerate(tail)]

            def before_tail(n):
                g, v = divmod(n, 4)
                if v == 0:
                    pe.wait_ge(outh_added, 7 * NB + g + 1)
                if v == 2:
                    pe.wait_ge(outg_added, NB + g + 1)

            stream(tail, None, lambda n: n % 2 == 0, lambda n: n % 2 == 1, before_tail)
            pe.wait_ge(outg_added, NB + NB // 2 + 1)
            pe.wait_ge(outh_added, 7 * NB + NB // 2 + 1)
            for g in range(NB):
                if g >= 4:
                    pe.wait_ge(s_copied, g - 3)
                for k in range(KT):
                    mm = nc.tensor.transpose(T[:, g % 4 // 2, g % 2, k * P:(k + 1) * P],
                                             outT[:, g * B + k * P:g * B + (k + 1) * P], ident[:, :])
                mm.then_inc(s_turned, 1)

        @block.scalar
        def _(act):
            act.dma_start(W_sb[:, :], W0).then_inc(const_loaded, 16)
            act.dma_start(b_bc[:, :], b0.partition_broadcast(P)).then_inc(const_loaded, 16)
            for c, (w, bb) in enumerate(((w_par, b_par), (w_chi, b_chi))):
                w2 = w.rearrange("(a p o) -> a p o", a=2, o=1)
                act.dma_start(w_left[:, c:c + 1], w2[0]).then_inc(const_loaded, 16)
                act.dma_start(w_right[:, c:c + 1], w2[1]).then_inc(const_loaded, 16)
                act.dma_start(bias2[:, c:c + 1], bb.partition_broadcast(P)).then_inc(const_loaded, 16)
            act.preload_act_table_set("natural_log_exp_and_others")
            act.sem_inc(half_free, 2)
            act.wait_ge(wt_psum, 1)
            nc.scalar.copy(WT[:, :], U[:, 0:P]).then_inc(wt_ready, 1)

            def log_pair(g):
                act.wait_ge(ln_in, g + 1)
                nc.scalar.activation(small[:, 21, 0:KT], small[:, 20, 0:KT], ACT.Ln, bias=1.0, scale=1.0)
                nc.scalar.activation(small[:, 22, 0:KT], small[:, 20, 0:KT], ACT.Ln, bias=1.0, scale=-1.0).then_inc(ln_out, 1)

            def score_copies(g):
                h = sv_halves_before(g)
                act.wait_ge(half_ready, h + 1)
                act.wait_ge(at_used, h + 2)
                nc.scalar.copy(tT, T[:, 0, 0, :]).then_inc(half_free, 1)
                act.wait_ge(half_ready, h + 2)
                nc.scalar.copy(left_par_bc[:, g * B:(g + 1) * B], T[:, 1, 0, :]).then_inc(half_free, 1)
                act.wait_ge(half_ready, h + 3)
                nc.scalar.copy(left_chi_bc[:, g * B:(g + 1) * B], T[:, 0, 0, :]).then_inc(half_free, 1)
                act.wait_ge(half_ready, h + 4)
                nc.scalar.copy(right[:, g * KT:(g + 1) * KT, :], T[:, 1, 0, 0:2 * KT].rearrange("p (k c) -> p k c", c=2))\
                    .then_inc(half_free, 1)

            for pan in panels:
                if not pan.segments:
                    continue
                G, i = pan.G, pan.index
                for seg in pan.segments:
                    h0 = halves_before(pan, seg)
                    nb = len(seg.bs)

                    def run(j):
                        for i2 in range(2 * nb):
                            act.wait_ge(half_ready, h0 + i2 + 1 + 2 * nb * j)
                            act.wait_ge(at_used, h0 + i2 + 2 + 2 * nb * j)
                            nc.scalar.copy(at[:, i2 % 2, :, :], T[:, i2 % 2, :, :]).then_inc(half_free, 1)

                    each_run(act, seg, run)
                    if pan.phase == 2 and seg is pan.segments[0] and G >= 2:
                        score_copies(G - 2)
                if pan.phase == 1:
                    act.wait_ge(acc_done, i + 1)
                    nc.scalar.copy(outT[:, G * B:(G + 1) * B], acc[i % 2][:, :]).then_inc(acc_stored, 1)
                elif G >= 1:
                    log_pair(G - 1)
            score_copies(NB - 2)
            log_pair(NB - 1)
            score_copies(NB - 1)
            act.drain().then_inc(layer0_over, 1)
            act.wait_ge(layer0_over, 4)

            def sigmoids(d, O, C, half, unit):
                act.wait_ge(par_done, unit + 1)
                act.sem_inc(act_turns, 1)
                for k in range(2):
                    c = C * KT + 2 * half + k
                    a = nc.scalar.activation(sig_par[:, d % 2, k, :], left_par_bc[:, bass.ts(O, B)], ACT.Sigmoid,
                                             bias=right[:, c, 0:1])
                a.then_inc(par_sig, 1)
                act.wait_ge(mixed, unit + 1)
                act.sem_inc(act_turns, 1)
                for k in range(2):
                    c = C * KT + 2 * half + k
                    a = nc.scalar.activation(chi[:, d % 3, k, :], left_chi_bc[:, bass.ts(O, B)], ACT.Sigmoid,
                                             bias=right[:, c, 1:2])
                a.then_inc(chi_sig, 1)

            with act.Fori(0, NB) as G:
                for r, slot, use, unit in positions(G):
                    H = (G + r) % NB if r else G
                    d = 4 * r - 2 if r else 0
                    if r:
                        for v in range(2):
                            sigmoids(d + v, H, G, v, unit + v)
                        for v in range(2):
                            sigmoids(d + 2 + v, G, H, v, unit + 2 + v)
                    else:
                        for v in range(2):
                            sigmoids(v, G, G, v, unit + v)
            for g in range(NB // 2):
                H, d = g + NB // 2, 4 * g
                for v in range(2):
                    sigmoids(d + v, H, g, v, TAIL_UNIT + d + v)
                for v in range(2):
                    sigmoids(d + 2 + v, g, H, v, TAIL_UNIT + d + 2 + v)
            for g in range(NB):
                act.wait_ge(s_turned, g + 1)
                nc.scalar.copy(s_all[:, g, :], T[:, g % 4 // 2, g % 2, :]).then_inc(s_copied, 1)
            act.wait_ge(norm_in, 1)
            nc.scalar.activation(fin[:, 6, :], fin[:, 5, :], ACT.Tanh).then_inc(tanh_out, 1)

        @block.gpsimd
        def _(pool):
            pool.sem_inc(chi_done, 5)
            nc.gpsimd.memset(ident[:, :], 0.0).then_inc(zero_ready, 1)
            pool.wait_ge(zero_ready, 1)
            nc.gpsimd.affine_select(out=ident[:, :], in_=ident[:, :], compare_op=ALU.not_equal, fill=1.0, base=0,
                                    pattern=[[-1, P]], channel_multiplier=1).then_inc(const_ready, 1)
            nc.gpsimd.memset(outT[:, 0:B], 0.0).then_inc(outT_zeroed, 1)

            def centre(g):
                s = g % 2
                pool.wait_ge(mean_ready, g + 1)
                if g >= 2:
                    pool.wait_ge(y_done, g - 1)
                x3 = x_buf[:, s, :].rearrange("p (m d) -> p m d", m=KT)
                c3 = cen_buf[:, s, :].rearrange("p (m d) -> p m d", m=KT)
                nc.gpsimd.tensor_tensor(c3, x3, small[:, s, 0:KT].unsqueeze(2).to_broadcast([P, KT, P]), ALU.subtract)\
                    .then_inc(pool_step, 1)
                pool_steps[0] += 1
                pool.wait_ge(pool_step, pool_steps[0])
                nc.gpsimd.tensor_tensor(sq_buf[:, s, :], cen_buf[:, s, :], cen_buf[:, s, :], ALU.mult).then_inc(centred, 1)

            def y_copies(pan, seg):
                def run(j):
                    for n, b in enumerate(seg.bs):
                        ys = (seg.blocks + n) % 2
                        H = 4 * (seg.j0 + j) + b
                        if pan.phase == 1:
                            pool.wait_ge(y_done, H + 1)
                        pool.wait_ge(at_used, halves_before(pan, seg) + 2 * n + 1 + 2 * len(seg.bs) * j)
                        nc.gpsimd.tensor_copy(y_slot[:, ys, :], y_sb[:, H, :]).then_inc(y_copied[ys], 1)
                each_run(pool, seg, run)

            centre(0)
            for pan in pass1:
                G = pan.G
                if G == 0:
                    centre(1)
                for n, seg in enumerate(pan.segments):
                    y_copies(pan, seg)
                    if n == 0 and G + 1 < NB:
                        centre(G + 1)

            def store_x1(g):
                pool.wait_ge(x1_ready, g + 1)
                pool.dma_start(x1_v[g], x1_buf[:, g % 2, :].rearrange("p (m d) -> p m d", m=KT)).then_inc(x1_stored[g % 2], 16)

            def store_t(g):
                pool.wait_ge(t_ready, g + 1)
                pool.dma_start(t_v[g], t_buf[:, g % 2, :].rearrange("p (m d) -> p m d", m=KT)).then_inc(t_stored[g % 2], 16)

            def clear(g):
                pool.wait_ge(z_done, g + 1)
                nc.gpsimd.memset(outT[:, g * B:(g + 1) * B], 0.0).then_inc(outT_zeroed, 1)

            pool.wait_ge(y_done, NB)
            for pan in pass2:
                G = pan.G
                s = G % 2
                pool.wait_ge(x_loaded[s], 16 * (NB // 2 + G // 2 + 1))
                x3 = x_buf[:, s, :].rearrange("p (m d) -> p m d", m=KT)
                nc.gpsimd.tensor_tensor(x3, x3, b_bc[:, :].unsqueeze(1).to_broadcast([P, KT, P]), ALU.add).then_inc(xb_ready, 1)
                for seg in pan.segments:
                    y_copies(pan, seg)
                if G >= 1:
                    clear(G - 1)
                    store_x1(G - 1)
                if G >= 2:
                    store_t(G - 2)
            clear(NB - 1)
            store_x1(NB - 1)
            store_t(NB - 2)
            store_t(NB - 1)
            pool.drain().then_inc(layer0_over, 1)
            pool.wait_ge(layer0_over, 4)

            def times_adj(d, slot, blk, half, unit, use=None):
                if use is not None:
                    pool.wait_ge(pair_loaded[slot], 64 * use + 64)
                pool.wait_ge(chi_sig, unit + 1)
                i = nc.gpsimd.tensor_tensor(chi[:, d % 3, :, :], chi[:, d % 3, :, :],
                                            ablk[:, 2 * slot + blk, 2 * half:2 * half + 2, :], ALU.mult)
                i.then_inc(chi_done, 1)

            with pool.Fori(0, NB) as G:
                for r, slot, use, unit in positions(G):
                    if r:
                        for v in range(4):
                            times_adj(4 * r - 2 + v, slot, v // 2, v % 2, unit + v, use if v == 0 else None)
                    else:
                        for v in range(2):
                            times_adj(v, slot, 1, v, unit + v, use if v == 0 else None)
            for g in range(NB // 2):
                for v in range(4):
                    times_adj(4 * g + v, g % 2, v // 2, v % 2, TAIL_UNIT + 4 * g + v,
                              TAIL_USE + g // 2 if v == 0 else None)
            sq4 = shared[:, 0:N].rearrange("p (g c) -> p g c", c=B)
            pool.wait_ge(outg_added, NB + NB // 2 + 1)
            for g in range(NB):
                pool.wait_ge(s_copied, g + 1)
                nc.gpsimd.tensor_tensor(sq4[:, g, :], s_all[:, g, :], s_all[:, g, :], ALU.mult).then_inc(s_squared, 1)

        @block.vector
        def _(dve):
            steps = [0]

            def step(i):
                steps[0] += 1
                i.then_inc(dve_step, 1)
                dve.wait_ge(dve_step, steps[0])

            def rsqrt(r, w, a, sh):
                step(nc.vector.tensor_scalar(a[sh].bitcast(U32), w[sh].bitcast(U32), 1, None, ALU.logical_shift_right))
                step(nc.vector.tensor_scalar(r[sh].bitcast(U32), a[sh].bitcast(U32), -1.0, float(RSQRT_SEED), ALU.mult, ALU.add))
                for _ in range(4):
                    step(nc.vector.tensor_tensor(a[sh], r[sh], r[sh], ALU.mult))
                    step(nc.vector.scalar_tensor_tensor(out=a[sh], in0=a[sh], scalar=-0.5, in1=w[sh], op0=ALU.mult, op1=ALU.mult))
                    step(nc.vector.scalar_tensor_tensor(out=r[sh], in0=a[sh], scalar=1.5, in1=r[sh], op0=ALU.add, op1=ALU.mult))

            def rows(a):
                return a.rearrange("p (m d) -> p m d", m=KT)

            def wide(a):
                return a.unsqueeze(2).to_broadcast([P, KT, P])

            for s in range(4):
                dve.sem_inc(rowsummed[s], 1)
            dve.sem_inc(par_done, 2)
            dve.sem_inc(mixed, 3)
            dve.sem_inc(outh_added, 1)
            dve.sem_inc(outg_added, 1)
            step(nc.vector.memset(zeros_bf[:, :], 0.0))
            dve.wait_ge(const_loaded, 16 * 8)
            for c in range(2):
                nc.vector.tensor_copy(w_left_rep[:, c, :], w_left[:, c:c + 1].to_broadcast([P, P])).then_inc(reps_ready, 1)

            def mean_of(g):
                s = g % 2
                dve.wait_ge(x_loaded[s], 16 * (g // 2 + 1))
                if g >= 2:
                    dve.wait_ge(centred, g - 1)
                if g:
                    dve.wait_ge(mean_ready, g)
                step(nc.vector.reduce_sum(small[:, 2, 0:KT], rows(x_buf[:, s, :]), AX))
                nc.vector.tensor_scalar(small[:, s, 0:KT], small[:, 2, 0:KT], 1.0 / D, None, ALU.mult).then_inc(mean_ready, 1)

            lo, hi = slice(0, KT), slice(KT, 2 * KT)
            both = (slice(None), slice(0, 2 * KT))
            low = (slice(None), lo)
            mean_of(0)
            for pan in pass1:
                G = pan.G
                if G + 1 < NB:
                    mean_of(G + 1)
                with dve.Fori(0, 4) as j:
                    for s in range(4):
                        dve.wait_ge(a_loaded[s], 16 * (4 * G + 1) + 16 * j)
                        nc.vector.reduce_sum(rowparts[:, :, bass.ds(4 * j + s, 1)], ablk[:, s, :, :], AX).then_inc(rowsummed[s], 1)
                w, r, a, mask = small[:, 3, :], small[:, 4, :], small[:, 5, :], small[:, 6, :]
                for s in range(4):
                    dve.wait_ge(rowsummed[s], 4 * (G + 1) + 1)
                step(nc.vector.reduce_sum(w[:, hi], rowparts[:, :, :], AX))
                dve.wait_ge(centred, G + 1)
                step(nc.vector.reduce_sum(w[:, lo], rows(sq_buf[:, G % 2, :]), AX))
                step(nc.vector.tensor_scalar(mask[:, hi], w[:, hi], 0.0, None, ALU.is_gt))
                step(nc.vector.tensor_scalar(w[:, lo], w[:, lo], 1.0 / D, LN_EPS, ALU.mult, ALU.add))
                step(nc.vector.tensor_scalar(w[:, hi], w[:, hi], MIN_NORM_SQ, None, ALU.max))
                rsqrt(r, w, a, both)
                step(nc.vector.tensor_tensor(dinv[:, G * KT:(G + 1) * KT], r[:, hi], mask[:, hi], ALU.mult))
                step(nc.vector.tensor_tensor(a[:, lo], r[:, lo], dinv[:, G * KT:(G + 1) * KT], ALU.mult))
                nc.vector.scalar_tensor_tensor(out=rows(y_sb[:, G, :]), in0=rows(cen_buf[:, G % 2, :]), scalar=0.0,
                                               in1=wide(a[:, lo]), op0=ALU.max, op1=ALU.mult).then_inc(y_done, 1)

            def layer0_rows(g):
                s = g % 2
                i = pass2[g].index
                dve.wait_ge(acc_done, i + 1)
                if g:
                    dve.wait_ge(acc_stored, g)
                else:
                    dve.wait_ge(outT_zeroed, 1)
                if g >= 2:
                    dve.wait_ge(u_done, g - 1)
                else:
                    dve.wait_ge(y_done, NB)
                nc.vector.tensor_tensor(z_buf[:, s, :], acc[i % 2][:, :], outT[:, g * B:(g + 1) * B], ALU.add).then_inc(z_done, 1)
                dve.wait_ge(u_done, g + 1)
                if g >= 2:
                    dve.wait_ge(x1_stored[s], 16 * (g // 2))
                x1 = x1_buf[:, s, :]
                nc.vector.tensor_tensor(rows(x1), rows(U[:, :]), wide(dinv[:, g * KT:(g + 1) * KT]), ALU.mult).then_inc(u_read, 1)
                dve.wait_ge(u_read, g + 1)
                dve.wait_ge(xb_ready, g + 1)
                nc.vector.tensor_tensor(x1, x1, x_buf[:, s, :], ALU.add).then_inc(x1_ready, 1)
                dve.wait_ge(x1_ready, g + 1)
                sm, mean, var, w, r, a = (small[:, n, 0:KT] for n in (7, 8, 9, 10, 11, 12))
                n2, rn, norm = (small[:, n, 0:KT] for n in (13, 14, 15))
                al = (slice(None), slice(None))
                step(nc.vector.reduce_sum(sm, rows(x1), AX))
                step(nc.vector.tensor_scalar(mean, sm, 1.0 / D, None, ALU.mult))
                step(nc.vector.tensor_tensor(rows(h_buf), rows(x1), wide(mean), ALU.subtract))
                step(nc.vector.tensor_tensor(hsq_buf, h_buf, h_buf, ALU.mult))
                step(nc.vector.reduce_sum(var, rows(hsq_buf), AX))
                step(nc.vector.tensor_scalar(w, var, 1.0 / D, LN_EPS, ALU.mult, ALU.add))
                rsqrt(r, w, a, al)
                step(nc.vector.scalar_tensor_tensor(out=rows(h_buf), in0=rows(h_buf), scalar=0.0, in1=wide(r),
                                                    op0=ALU.max, op1=ALU.mult))
                step(nc.vector.tensor_tensor(hsq_buf, h_buf, h_buf, ALU.mult))
                step(nc.vector.reduce_sum(n2, rows(hsq_buf), AX))
                step(nc.vector.tensor_scalar(n2, n2, MIN_NORM_SQ, None, ALU.max))
                rsqrt(rn, n2, a, al)
                step(nc.vector.tensor_tensor(norm, n2, rn, ALU.mult))
                nc.vector.tensor_scalar(small[:, 20, 0:KT], norm, ARTANH_MAX, None, ALU.min).then_inc(ln_in, 1)

            def tangent(g):
                s = g % 2
                n2, rn, f, x2, p, m = (small[:, n, 0:KT] for n in (13, 14, 16, 17, 18, 19))
                dve.wait_ge(ln_out, g + 1)
                step(nc.vector.tensor_tensor(f, small[:, 21, 0:KT], small[:, 22, 0:KT], ALU.subtract))
                step(nc.vector.scalar_tensor_tensor(out=f, in0=f, scalar=0.5, in1=rn, op0=ALU.mult, op1=ALU.mult))
                step(nc.vector.tensor_scalar(m, n2, SERIES_SQ, None, ALU.is_lt))
                step(nc.vector.tensor_scalar(x2, n2, SERIES_SQ, None, ALU.min))
                step(nc.vector.tensor_scalar(p, x2, 1.0 / 13, None, ALU.mult))
                for o in (11, 9, 7, 5, 3):
                    step(nc.vector.scalar_tensor_tensor(out=p, in0=p, scalar=1.0 / o, in1=x2, op0=ALU.add, op1=ALU.mult))
                step(nc.vector.scalar_tensor_tensor(out=p, in0=p, scalar=1.0, in1=f, op0=ALU.add, op1=ALU.subtract))
                step(nc.vector.tensor_tensor(p, p, m, ALU.mult))
                step(nc.vector.tensor_tensor(f, f, p, ALU.add))
                if g >= 2:
                    dve.wait_ge(t_stored[s], 16 * (g // 2))
                    dve.wait_ge(half_ready, sv_halves_before(g - 2) + 1)
                nc.vector.tensor_tensor(rows(t_buf[:, s, :]), rows(h_buf), wide(f), ALU.mult).then_inc(t_ready, 1)
                dve.wait_ge(t_ready, g + 1)

            for pan in pass2:
                layer0_rows(pan.G)
                tangent(pan.G)
            dve.wait_ge(half_free, HALVES0 + SV_HALVES * NB + 2)
            for c in range(2):
                step(nc.vector.tensor_scalar(right[:, :, c], right[:, :, c], bias2[:, c:c + 1], None, ALU.add))
            dve.wait_ge(outT_zeroed, NB + 1)
            dve.drain().then_inc(layer0_over, 1)
            dve.wait_ge(layer0_over, 4)

            def par(d, unit):
                dve.wait_ge(turned, unit + 1)
                dve.wait_ge(par_sig, unit + 1)
                nc.vector.tensor_tensor(T[:, d % 2, :, :], T[:, d % 2, :, :], sig_par[:, d % 2, :, :], ALU.mult).then_inc(par_done, 1)

            def add_chi(d, unit):
                dve.wait_ge(par_done, unit + 3)
                dve.wait_ge(chi_done, unit + 6)
                dve.wait_ge(unit_used, unit + 4)
                nc.vector.tensor_tensor(mix[:, d % 2, :, :], T[:, d % 2, :, :], chi[:, d % 3, :, :], ALU.add).then_inc(mixed, 1)

            def add_out(block_no, bank, done, used, h_before, g_before):
                dve.wait_ge(unit_used, used + 6)
                dve.wait_ge(outh_added, h_before + 1)
                dve.wait_ge(outg_added, g_before + 1)
                o = outT[:, bass.ts(block_no, B)]
                nc.vector.tensor_tensor(o, bank[:, :], o, ALU.add).then_inc(done, 1)

            outg, outh = acc[0], acc[1]
            par(0, 0)
            with dve.Fori(0, NB) as G:
                unit0 = UNITS_G * G
                for d in range(UNITS_G):
                    add_chi(d, unit0 + d)
                    par(d + 1 if d + 1 < UNITS_G else 0, unit0 + d + 1)
                    if d >= 2 and (d - 2) % 4 == 2:
                        r = (d - 2) // 4 + 1
                        add_out((G + r) % NB, outh, outh_added, unit0 + 4 * r - 1, 7 * G + r - 1, G)
                add_out(G, outg, outg_added, unit0 + UNITS_G - 1, 7 * G + 7, G)
            for g in range(NB // 2):
                for v in range(4):
                    d = 4 * g + v
                    add_chi(d, TAIL_UNIT + d)
                    if d + 1 < 2 * NB:
                        par(d + 1, TAIL_UNIT + d + 1)
                    if v == 2:
                        add_out(g + NB // 2, outh, outh_added, TAIL_UNIT + 4 * g + 1, 7 * NB + g, NB + g)
                add_out(g, outg, outg_added, TAIL_UNIT + 4 * g + 3, 7 * NB + g + 1, NB + g)

            sq4 = shared[:, 0:N].rearrange("p (g c) -> p g c", c=B)
            for g in range(NB):
                dve.wait_ge(s_squared, g + 1)
                step(nc.vector.reduce_sum(fin[:, 0, g * KT:(g + 1) * KT], rows(sq4[:, g, :]), AX))
            al = (slice(None), slice(None))
            step(nc.vector.tensor_scalar(fin[:, 1, :], fin[:, 0, :], MIN_NORM_SQ, None, ALU.max))
            rsqrt(fin[:, 2, :], fin[:, 1, :], fin[:, 3, :], al)
            nc.vector.tensor_tensor(fin[:, 5, :], fin[:, 1, :], fin[:, 2, :], ALU.mult).then_inc(norm_in, 1)
            dve.wait_ge(tanh_out, 1)
            step(nc.vector.scalar_tensor_tensor(out=fin[:, 7, :], in0=fin[:, 6, :], scalar=MAX_NORM, in1=fin[:, 2, :],
                                                op0=ALU.min, op1=ALU.mult))
            dve.wait_ge(x1_back, 16 * NB)
            for g in range(NB):
                for k in range(KT):
                    c = slice(k * P, (k + 1) * P)
                    i = nc.vector.scalar_tensor_tensor(out=s_all[:, g, c], in0=s_all[:, g, c],
                                                       scalar=fin[:, 7, g * KT + k:g * KT + k + 1],
                                                       in1=x1_all[:, g, c], op0=ALU.mult, op1=ALU.add)
                i.then_inc(fin_ready, 1)


_INS = ['x', 'adj', 'L0_gnn_W', 'L0_gnn_b', 'L1_gnn_w_par', 'L1_gnn_b_par', 'L1_gnn_w_chi', 'L1_gnn_b_chi']


def kernel(**inputs):
    import numpy as _np
    import concourse.bacc as _bacc
    from concourse import mybir as _mybir
    from concourse.bass_utils import run_bass_kernel_spmd as _run

    nc = _bacc.Bacc("TRN2", target_bir_lowering=False, num_devices=1)
    arrays, args = {}, []
    for name in _INS:
        a = _np.ascontiguousarray(inputs[name])
        arrays[f"in_{name}"] = a
        args.append(nc.dram_tensor(f"in_{name}", a.shape, _mybir.dt.from_np(a.dtype), kind="ExternalInput").ap())
    shape = arrays["in_x"].shape
    out = nc.dram_tensor("out_dram", shape, _mybir.dt.float32, kind="ExternalOutput").ap()
    x1 = nc.dram_tensor("x1_dram", shape, _mybir.dt.float32, kind="Internal").ap()
    t = nc.dram_tensor("t_dram", shape, _mybir.dt.float32, kind="Internal").ap()
    gnn_kernel(nc, *args, out, x1, t)
    r = _run(nc, [arrays], core_ids=[0])
    return r.results[0]["out_dram"]
```

```python
import concourse.bass as bass
from concourse import mybir
from contextlib import ExitStack

F32 = mybir.dt.float32
F32R = mybir.dt.float32r
U32 = mybir.dt.uint32
ALU = mybir.AluOpType
ACT = mybir.ActivationFunctionType
AX = mybir.AxisListType.X

P = 128
KT = 4
B = P * KT
LN_EPS = 1e-5
ARTANH_MAX = 1.0 - 1e-7
MIN_NORM_SQ = 1e-30
MAX_NORM = 1.0 - 1e-5
SERIES_SQ = 0.0625
RSQRT_SEED = 0x5F3759DF


class Segment:

    def __init__(self, G, n, items, blocks, a_use, turned):
        self.G, self.n, self.items, self.blocks = G, n, items, blocks
        self.prods = [i for i in items if i[3]]
        self.nprod = len(self.prods)
        self.a_use, self.turned = dict(a_use), dict(turned)


def t_after(n):
    return min(2, n - 1)


def u_after(n):
    return 0 if n <= 4 else 1


class Panel:

    def __init__(self, phase, G, index):
        self.phase, self.G, self.index = phase, G, index
        self.segments = []


def plan_panels(NB):
    PASS_ORDER = {1: list(range(NB)), 2: [14, 15, 0, 1, 12, 13, 10, 11, 8, 9, 6, 7, 4, 5, 2, 3]}
    panels = []
    blocks = index = slot = 0
    a_use = dict.fromkeys(range(4), 0)
    turned = dict.fromkeys(range(4), 0)
    for phase in (1, 2):
        for G in PASS_ORDER[phase]:
            pan = Panel(phase, G, index)
            if phase == 1:
                if G <= 8:
                    fours = [0] * (NB // 4 - (G + 1) // 2) + [2] * (G // 2) + [1] * (G % 2)
                elif G <= 12:
                    fours = [2] * (12 - G) + [3] * (G - 8)
                else:
                    fours = [4] * (G - 12) + [3] * (NB - G)
                todo, p0, m0 = [], 0, G
                while fours:
                    k = fours[0]
                    n = 1 if k % 2 else fours.count(k)
                    del fours[:n]
                    take = [(p0 + i, k, True) for i in range(k)]
                    rest = [(m0 + i, 4 - k, False) for i in range(4 - k)]
                    if k == 2:
                        take, rest = [take[0], rest[0], take[1], rest[1]], []
                    elif k == 3:
                        take, rest = take[:2] + rest + take[2:], []
                    todo.append((n, take + rest))
                    p0 += k * n
                    m0 += (4 - k) * n
            else:
                quads, rest = divmod(NB - G, 4)
                todo = [(1, [(G + i, 0, True) for i in range(rest)])] if rest else []
                todo.append((min(quads, 1), [(G + rest + i, 0, True) for i in range(4)]))
                todo.append((quads - 1, [(G + rest + 4 + i, 4, True) for i in range(4)]))
            for n, what in todo:
                if n < 1:
                    continue
                items = [((slot + i) % 4, *w) for i, w in enumerate(what)]
                seg = Segment(G, n, items, blocks, a_use, turned)
                pan.segments.append(seg)
                slot += len(items)
                blocks += n * seg.nprod
                for b, _, _, multiplied in items:
                    a_use[b] += n
                    turned[b] += n * multiplied
            pan.multiplies = any(g.nprod for g in pan.segments)
            pan.blocks_end = blocks
            index += pan.multiplies
            panels.append(pan)
    return panels, turned


def gnn_kernel(nc, x, adj, W0, b0, w_par, b_par, w_chi, b_chi, out, x1_dram, t_dram):
    N, D = x.shape
    NB = N // B
    NT = N // P
    assert D == P and NB == 16

    adj_v = adj.rearrange("(g m p) (h c) -> g h p m c", m=KT, p=P, c=B)
    x_v = x.rearrange("(g m p) d -> g p m d", m=KT, p=P)
    out_v = out.rearrange("(g m p) d -> g p m d", m=KT, p=P)
    x1_v = x1_dram.rearrange("(g m p) d -> g p m d", m=KT, p=P)
    t_v = t_dram.rearrange("(g m p) d -> g p m d", m=KT, p=P)

    panels, turned_all = plan_panels(NB)
    pass1 = [p for p in panels if p.phase == 1]
    pass2 = [p for p in panels if p.phase == 2]
    pairs = [p.G // 2 * 2 for p in pass2[::2]]

    ctx = ExitStack()
    with ctx:
        def sb(name, shape, dt=F32):
            return ctx.enter_context(nc.sbuf_tensor(name, shape, dt))

        def sem(name):
            return ctx.enter_context(nc.semaphore(name))

        left_par_bc = sb("left_par_bc", [P, N])
        left_chi_bc = sb("left_chi_bc", [P, N])
        outT = sb("outT", [P, N])
        ablk = sb("ablk", [P, 4, KT, B])
        shared = sb("shared", [P, N])
        temps = sb("temps", [P, 8 * B])
        at_hi = sb("at_hi", [P, KT, B], F32R)
        at_lo = sb("at_lo", [P, KT, B], F32R)
        y_hi = sb("y_hi", [P, 2, B], F32R)
        y_lo = sb("y_lo", [P, 2, B], F32R)
        right = sb("right", [P, NT, 2])
        dinv = sb("dinv", [P, NT])
        rowparts = sb("rowparts", [P, 2, KT, NB])
        ident = sb("ident", [P, P])
        W_sb = sb("W_sb", [P, P])
        WT = sb("WT", [P, P])
        b_bc = sb("b_bc", [P, P])
        w_left = sb("w_left", [P, 2])
        w_right = sb("w_right", [P, 2])
        w_left_rep = sb("w_left_rep", [P, 2, P])
        bias2 = sb("bias2", [P, 2])
        small = sb("small", [P, 24, 2 * KT])
        fin = sb("fin", [P, 7, NT])

        y_sb = shared[:, :].rearrange("p (g c) -> p g c", c=B)
        x_buf = temps[:, 0:2 * B].rearrange("p (r c) -> p r c", r=2)
        cen_buf = temps[:, 2 * B:4 * B].rearrange("p (r c) -> p r c", r=2)
        sq_buf = temps[:, 4 * B:6 * B].rearrange("p (r c) -> p r c", r=2)
        t_buf = temps[:, 6 * B:8 * B].rearrange("p (r c) -> p r c", r=2)
        h_buf = cen_buf
        hsq_buf = sq_buf
        sig_par = shared[:, 0:6 * B].rearrange("p (r k c) -> p r k c", r=3, k=2)
        chi = shared[:, 6 * B:16 * B].rearrange("p (r k c) -> p r k c", r=5, k=2)
        mix = temps[:, 0:4 * B].rearrange("p (r k c) -> p r k c", r=2, k=2)
        tg = [temps[:, (4 + 2 * s) * B:(6 + 2 * s) * B].rearrange("p (k c) -> p k c", k=2) for s in range(2)]
        x1_all = left_par_bc[:, :].rearrange("p (g c) -> p g c", c=B)
        s_all = ablk[:, :, :, :].rearrange("p a m c -> p (a m) c")

        T = ctx.enter_context(nc.psum_tensor("T", [P, 3, 2, B], F32))
        acc = [ctx.enter_context(nc.psum_tensor(f"acc{i}", [P, B], F32)) for i in range(2)]
        TQ = [T[:, k // 2, k % 2, :] for k in range(KT)]
        U = T[:, 2, 0, :]
        V = T[:, 2, 1, :]
        discard = [U, V, t_buf[:, 0, :], t_buf[:, 1, :]]

        a_loaded = [sem(f"a_loaded{s}") for s in range(4)]
        rowsummed_dve = [sem(f"rowsummed_dve{s}") for s in range(4)]
        rowsummed_act = [sem(f"rowsummed_act{s}") for s in range(4)]
        transposed = [sem(f"transposed{s}") for s in range(4)]
        turned_tile = sem("turned_tile")
        hi_done = sem("hi_done")
        lo_done = sem("lo_done")
        at_used = sem("at_used")
        y_hi_done = sem("y_hi_done")
        y_split = sem("y_split")
        sv_ready = sem("sv_ready")
        sv_read = sem("sv_read")
        x_loaded = [sem(f"x_loaded{s}") for s in range(2)]
        mean_ready = sem("mean_ready")
        centred = sem("centred")
        y_done = sem("y_done")
        acc_stored = sem("acc_stored")
        const_loaded = sem("const_loaded")
        const_ready = sem("const_ready")
        wt_psum = sem("wt_psum")
        wt_ready = sem("wt_ready")
        zero_ready = sem("zero_ready")
        reps_ready = sem("reps_ready")
        z_done = sem("z_done")
        u_done = sem("u_done")
        u_read = sem("u_read")
        xb_ready = sem("xb_ready")
        x1_ready = sem("x1_ready")
        norm_start = sem("norm_start")
        ln_in = sem("ln_in")
        ln_out = sem("ln_out")
        t_ready = sem("t_ready")
        outT_zeroed = sem("outT_zeroed")
        x1_stored = sem("x1_stored")
        t_stored = sem("t_stored")
        layer0_over = sem("layer0_over")
        dve_step = sem("dve_step")
        act_turns = sem("act_turns")
        sp_turns = sem("sp_turns")
        pool_turns = sem("pool_turns")
        pair_loaded = [sem(f"pair_loaded{s}") for s in range(2)]
        pair_t_loaded = [sem(f"pair_t_loaded{s}") for s in range(2)]
        turned = sem("turned")
        par_sig = sem("par_sig")
        chi_sig = sem("chi_sig")
        chi_done = sem("chi_done")
        par_done = sem("par_done")
        mixed = sem("mixed")
        unit_used = sem("unit_used")
        outh_added = sem("outh_added")
        outg_added = sem("outg_added")
        x1_back = sem("x1_back")
        s_turned = sem("s_turned")
        s_copied = sem("s_copied")
        s_squared = sem("s_squared")
        norm_in = sem("norm_in")
        tanh_out = sem("tanh_out")
        scale_ready = sem("scale_ready")
        s_scaled = sem("s_scaled")
        fin_ready_dve = sem("fin_ready_dve")
        fin_ready_pool = sem("fin_ready_pool")
        out_stored = sem("out_stored")

        block = ctx.enter_context(nc.Block())

        PAIRS = NB // 2

        def each_run(eng, seg, body):
            if seg.n > 1:
                with eng.Fori(0, seg.n) as j:
                    body(j)
            else:
                body(0)

        def positions(G):
            for i in range(NB // 2):
                yield i, (i + 1) % (NB // 2), i % 2, G * (NB // 4) + i // 2, G * 30 + 4 * i

        UNITS_G = 30
        TAIL_UNIT = UNITS_G * NB
        TAIL_USE = NB * (NB // 4)

        @block.sync
        def _(sp):
            def load_x(g):
                sp.dma_start(x_buf[:, g % 2, :].rearrange("p (m d) -> p m d", m=KT), x_v[g]).then_inc(x_loaded[g % 2], 16)

            load_x(0)
            for pan in pass1:
                G = pan.G
                for seg in pan.segments:
                    def run(j):
                        for b, H0, step, multiplied in seg.items:
                            sp.wait_ge(rowsummed_dve[b], seg.a_use[b] + 1 + j)
                            sp.sem_inc(sp_turns, 1)
                            sp.wait_ge(rowsummed_act[b], 2 * seg.a_use[b] + 1 + 2 * j)
                            sp.sem_inc(sp_turns, 1)
                            sp.wait_ge(transposed[b], seg.turned[b] + 1 + (j if multiplied else 0))
                            sp.dma_start(ablk[:, b, :, :], adj_v[G, H0 + step * j]).then_inc(a_loaded[b], 16)
                    each_run(sp, seg, run)
                    if seg is pan.segments[0] and G + 1 < NB:
                        if G >= 1:
                            sp.wait_ge(centred, G)
                        load_x(G + 1)
            first_use = set(range(4))
            for q, pan in enumerate(pass2):
                G = pan.G
                for seg in pan.segments:
                    def run(j):
                        for b, H0, step, _ in seg.items:
                            if b in first_use:
                                first_use.remove(b)
                                sp.wait_ge(rowsummed_dve[b], 4 * NB + 1)
                                sp.wait_ge(rowsummed_act[b], 8 * NB + 1)
                            sp.wait_ge(transposed[b], seg.turned[b] + 1 + j)
                            sp.dma_start(ablk[:, b, :, :], adj_v[G, H0 + step * j]).then_inc(a_loaded[b], 16)
                    each_run(sp, seg, run)
                if q % 2:
                    p = q // 2
                    if p:
                        sp.wait_ge(x1_stored, 16 * p)
                        sp.wait_ge(norm_start, p)
                    else:
                        sp.wait_ge(centred, NB)
                    load_x(pairs[p])
                    load_x(pairs[p] + 1)

            for s in range(4):
                sp.wait_ge(transposed[s], turned_all[s] + 1)

            def tile_of(a):
                return a.rearrange("p (m d) -> p m d", m=KT)

            def load_pair(G, H, slot, last_unit):
                sp.wait_ge(turned, last_unit + 6)
                sp.wait_ge(chi_done, last_unit + 6)
                if H is None:
                    sp.dma_start(ablk[:, 2 * slot + 1, :, :], adj_v[G, G]).then_inc(pair_loaded[slot], 32)
                    sp.wait_ge(unit_used, last_unit + 6)
                    sp.dma_start(tile_of(tg[slot][:, 0, :]), t_v[G]).then_inc(pair_t_loaded[slot], 32)
                else:
                    sp.dma_start(ablk[:, 2 * slot + 1, :, :], adj_v[H, G]).then_inc(pair_loaded[slot], 16)
                    sp.dma_start(ablk[:, 2 * slot, :, :], adj_v[G, H]).then_inc(pair_loaded[slot], 16)
                    sp.wait_ge(unit_used, last_unit + 6)
                    sp.dma_start(tile_of(tg[slot][:, 0, :]), t_v[G]).then_inc(pair_t_loaded[slot], 16)
                    sp.dma_start(tile_of(tg[slot][:, 1, :]), t_v[H]).then_inc(pair_t_loaded[slot], 16)

            with sp.Fori(0, NB) as G:
                for i, r, slot, _, unit in positions(G):
                    load_pair(G, (G + r) % NB if r else None, slot, unit - (5 if i else 3))
            for g in range(NB // 2):
                load_pair(g, g + NB // 2, g % 2, TAIL_UNIT + 4 * g - (5 if g else 3))
            sp.wait_ge(par_sig, TAIL_UNIT + 2 * NB)
            for g in range(NB):
                sp.dma_start(tile_of(x1_all[:, g, :]), x1_v[g]).then_inc(x1_back, 16)
            for g in range(NB):
                if g % 3 == 2:
                    sp.wait_ge(fin_ready_pool, g // 3 + 1)
                else:
                    sp.wait_ge(fin_ready_dve, g + 1 - g // 3)
                sp.dma_start(out_v[g], tile_of(s_all[:, g, :])).then_inc(out_stored, 16)
            sp.wait_ge(out_stored, 16 * NB)

        @block.tensor
        def _(pe):
            for s in range(4):
                pe.sem_inc(transposed[s], 1)
            pe.sem_inc(at_used, 5)
            pe.sem_inc(turned, 5)
            pe.wait_ge(const_loaded, 16 * 8)
            pe.wait_ge(const_ready, 1)
            nc.tensor.transpose(U[:, 0:P], W_sb[:, :], ident[:, :]).then_inc(wt_psum, 1)
            pe.wait_ge(reps_ready, 2)

            def u_parts(p):
                pe.wait_ge(z_done, 2 * p + 2)
                if p:
                    pe.wait_ge(sv_read, 7 * p)
                for g, bank in ((pairs[p], U), (pairs[p] + 1, V)):
                    for k in range(KT):
                        c = slice(k * P, (k + 1) * P)
                        mm = nc.tensor.matmul(bank[:, c], outT[:, g * B + k * P:g * B + (k + 1) * P], WT[:, :],
                                              start=True, stop=True)
                    mm.then_inc(u_done, 1)

            def turn_t(p):
                pe.wait_ge(t_ready, p + 1)
                pe.wait_ge(u_read, 2 * p + 2)
                for s, bank in ((0, U), (1, V)):
                    for k in range(KT):
                        c = slice(k * P, (k + 1) * P)
                        mm = nc.tensor.transpose(bank[:, c], t_buf[:, s, c], ident[:, :])
                    mm.then_inc(sv_ready, 1)

            def score_vectors(p, spare):
                tT = [outT[:, g * B:(g + 1) * B] for g in (pairs[p], pairs[p] + 1)]
                pe.wait_ge(sv_read, 7 * p + 2)
                pe.wait_ge(z_done, min(2 * p + 3, NB))
                nc.tensor.matmul(U[:, :], w_left_rep[:, 0, :], tT[0], start=True, stop=True).then_inc(sv_ready, 1)
                nc.tensor.matmul(V[:, :], w_left_rep[:, 0, :], tT[1], start=True, stop=True).then_inc(sv_ready, 1)
                nc.tensor.matmul(spare[:, :], w_left_rep[:, 1, :], tT[0], start=True, stop=True).then_inc(sv_ready, 1)
                pe.wait_ge(sv_read, 7 * p + 3)
                nc.tensor.matmul(U[:, :], w_left_rep[:, 1, :], tT[1], start=True, stop=True).then_inc(sv_ready, 1)
                pe.wait_ge(sv_read, 7 * p + 4)
                for s in range(2):
                    for k in range(KT):
                        c = 2 * (s * KT + k)
                        mm = nc.tensor.matmul(V[:, c:c + 2], tT[s][:, k * P:(k + 1) * P], w_right[:, :],
                                              start=True, stop=True)
                mm.then_inc(sv_ready, 1)

            def turn0(seg, j, t):
                n, k = divmod(t, KT)
                b = seg.prods[n][0]
                if k == 0:
                    pe.wait_ge(a_loaded[b], 16 * (seg.a_use[b] + 1) + 16 * j)
                pe.wait_ge(lo_done, KT * seg.blocks + t + 1 + KT * seg.nprod * j)
                for m in range(KT):
                    mm = nc.tensor.transpose(TQ[k][:, m * P:(m + 1) * P], ablk[:, b, m, k * P:(k + 1) * P], ident[:, :])
                mm.then_inc(turned_tile, 1)

            def multiply0(bank, seg, j, t, start, stop):
                n, k = divmod(t, KT)
                ys = (seg.blocks + n) % 2
                if k == 0:
                    pe.wait_ge(y_split, seg.blocks + n + 1 + seg.nprod * j)
                pe.wait_ge(lo_done, KT * seg.blocks + t + 5 + KT * seg.nprod * j)
                c = slice(k * P, (k + 1) * P)
                mm = nc.tensor.matmul(bank[:, :], y_hi[:, ys, c], at_hi[:, k, :], start=start, stop=False)
                if k == KT - 1 - AHEAD:
                    mm.then_inc(transposed[seg.prods[n][0]], 1)
                nc.tensor.matmul(bank[:, :], y_hi[:, ys, c], at_lo[:, k, :], start=False, stop=False)
                nc.tensor.matmul(bank[:, :], y_lo[:, ys, c], at_hi[:, k, :], start=False, stop=stop)\
                    .then_inc(at_used, 1)

            AHEAD = KT - 1

            def repetition(bank, seg, j, next_seg, next_j, start=False, stop=False, after_block=None):
                nt = KT * seg.nprod
                for t in range(nt):
                    if t + AHEAD < nt:
                        turn0(seg, j, t + AHEAD)
                    elif next_seg:
                        turn0(next_seg, next_j, t + AHEAD - nt)
                    multiply0(bank, seg, j, t, start and t == 0, stop and t == nt - 1)
                    if after_block and t % KT == KT - 1:
                        after_block(t // KT)

            stream0 = [(pan, seg) for pan in panels for seg in pan.segments if seg.nprod]
            for t in range(AHEAD):
                turn0(stream0[0][1], 0, t)
            for n, (pan, seg) in enumerate(stream0):
                i, size = pan.index, NB - pan.G
                q = i - (NB - 1)
                bank = acc[i % 2]
                first = n == 0 or stream0[n - 1][0] is not pan
                last = n + 1 == len(stream0) or stream0[n + 1][0] is not pan
                next_seg = stream0[n + 1][1] if n + 1 < len(stream0) else None
                if first:
                    before = 0
                    if i >= 2:
                        if i - 2 < NB - 1:
                            pe.wait_ge(acc_stored, i - 1)
                        else:
                            pe.wait_ge(z_done, i - 2 - (NB - 1) + 1)
                    if pan.phase == 2 and q >= 4:
                        pe.wait_ge(sv_read, 7 * ((q - 4) // 2) + 5)

                def after_block(b):
                    if q >= 2 and q % 2 == 0 and before + b == u_after(size):
                        if q == 2:
                            for s in range(4):
                                pe.wait_ge(rowsummed_act[s], 8 * NB + 1)
                        u_parts(q // 2 - 1)
                    if q >= 3 and q % 2 and before + b == t_after(size):
                        turn_t((q - 3) // 2)

                pause = last and next_seg and stream0[n + 1][0].segments[0] is not next_seg
                first_j = 0
                if seg.n > 1:
                    if first:
                        repetition(bank, seg, 0, seg, 1, start=True)
                        first_j = 1
                    if seg.n - 1 > first_j:
                        with pe.Fori(first_j, seg.n - 1) as j:
                            repetition(bank, seg, j, seg, j + 1)
                repetition(bank, seg, seg.n - 1, None if pause else next_seg, 0, start=first and seg.n == 1, stop=last,
                           after_block=after_block if pan.phase == 2 and seg.n == 1 else None)
                before += seg.nprod * seg.n
                if pause:
                    for t in range(AHEAD):
                        turn0(next_seg, 0, t)
                if pan.phase == 2 and q >= 3 and q % 2 and last:
                    score_vectors((q - 3) // 2, acc[(i + 1) % 2])
            u_parts(PAIRS - 1)
            turn_t(PAIRS - 1)
            score_vectors(PAIRS - 1, acc[(i + 1) % 2])
            pe.drain().then_inc(layer0_over, 1)
            pe.wait_ge(layer0_over, 4)

            pe.sem_inc(unit_used, 5)
            outg, outh = acc[0], acc[1]

            def turn(d, slot, blk, half, unit, first_of_use=None):
                if first_of_use is not None:
                    pe.wait_ge(pair_loaded[slot], 32 * first_of_use + 32)
                pe.wait_ge(mixed, unit + 3)
                for k in range(2):
                    for m in range(KT):
                        c = (2 * half + k) * P
                        mm = nc.tensor.transpose(T[:, d % 3, k, m * P:(m + 1) * P], ablk[:, 2 * slot + blk, m, c:c + P],
                                                 ident[:, :])
                mm.then_inc(turned, 1)

            def multiply(d, slot, which, half, unit, bank, start, stop, first_of_use=None):
                if first_of_use is not None:
                    pe.wait_ge(pair_t_loaded[slot], 32 * first_of_use + 32)
                pe.wait_ge(mixed, unit + 6)
                for k in range(2):
                    c = (2 * half + k) * P
                    mm = nc.tensor.matmul(bank[:, :], tg[slot][:, which, c:c + P], mix[:, d % 2, k, :],
                                          start=start and k == 0, stop=stop and k == 1)
                mm.then_inc(unit_used, 1)

            def units_of(d, slot, use, unit0, diagonal):
                if diagonal:
                    for half in range(2):
                        yield d + half, slot, 1, half, use if half == 0 else None, 0, outg, unit0 + half
                else:
                    for v in range(4):
                        o_is_g = v >= 2
                        yield (d + v, slot, 0 if o_is_g else 1, v % 2, use if v == 0 else None,
                               1 if o_is_g else 0, outg if o_is_g else outh, unit0 + v)

            def stream(units, nxt, starts, stops, before):
                for n, (d, slot, blk, half, fu, which, bank, unit) in enumerate(units):
                    if n + 2 < len(units):
                        d2, s2, blk2, half2, fu2, _, _, unit2 = units[n + 2]
                        turn(d2, s2, blk2, half2, unit2, fu2)
                    elif nxt:
                        nxt(n + 2 - len(units))
                    before(n)
                    multiply(d, slot, which, half, unit, bank, starts(n), stops(n), fu)

            turn(0, 0, 1, 0, 0, 0)
            turn(1, 0, 1, 1, 1)
            with pe.Fori(0, NB) as G:
                units = [u for i, r, slot, use, unit0 in positions(G) for u in units_of(4 * i, slot, use, unit0, r == 0)]

                def before(n):
                    if n == 2:
                        pe.wait_ge(outg_added, G + 1)
                    elif n % 4 == 0 and n < 28:
                        pe.wait_ge(outh_added, 7 * G + n // 4 + 1)

                stream(units, lambda v: turn(v, 0, 1, v, UNITS_G * G + UNITS_G + v,
                                             (NB // 4) * G + NB // 4 if v == 0 else None),
                       lambda n: n == 2 or (n % 4 == 0 and n < 28),
                       lambda n: n == UNITS_G - 1 or (n % 4 == 1 and n < 28), before)
            tail = [u for g in range(NB // 2)
                    for u in units_of(4 * g, g % 2, TAIL_USE + g // 2, TAIL_UNIT + 4 * g, False)]

            def before_tail(n):
                g, v = divmod(n, 4)
                if v == 0:
                    pe.wait_ge(outh_added, 7 * NB + g + 1)
                if v == 2:
                    pe.wait_ge(outg_added, NB + g + 1)

            stream(tail, None, lambda n: n % 2 == 0, lambda n: n % 2 == 1, before_tail)
            pe.wait_ge(outg_added, NB + NB // 2 + 1)
            pe.wait_ge(outh_added, 7 * NB + NB // 2 + 1)
            for g in range(NB):
                if g >= 4:
                    pe.wait_ge(s_copied, g - 3)
                for k in range(KT):
                    mm = nc.tensor.transpose(T[:, g % 4 // 2, g % 2, k * P:(k + 1) * P],
                                             outT[:, g * B + k * P:g * B + (k + 1) * P], ident[:, :])
                mm.then_inc(s_turned, 1)

        @block.scalar
        def _(act):
            act.dma_start(W_sb[:, :], W0).then_inc(const_loaded, 16)
            act.dma_start(b_bc[:, :], b0.partition_broadcast(P)).then_inc(const_loaded, 16)
            for c, (w, bb) in enumerate(((w_par, b_par), (w_chi, b_chi))):
                w2 = w.rearrange("(a p o) -> a p o", a=2, o=1)
                act.dma_start(w_left[:, c:c + 1], w2[0]).then_inc(const_loaded, 16)
                act.dma_start(w_right[:, c:c + 1], w2[1]).then_inc(const_loaded, 16)
                act.dma_start(bias2[:, c:c + 1], bb.partition_broadcast(P)).then_inc(const_loaded, 16)
            act.preload_act_table_set("natural_log_exp_and_others")
            for s in range(4):
                act.sem_inc(rowsummed_act[s], 1)
            act.wait_ge(wt_psum, 1)
            nc.scalar.copy(WT[:, :], U[:, 0:P]).then_inc(wt_ready, 1)
            act.wait_ge(wt_ready, 1)

            def logarithms(p):
                act.wait_ge(ln_in, p + 1)
                nc.scalar.activation(small[:, 21, :], small[:, 20, :], ACT.Ln, bias=1.0, scale=1.0)
                nc.scalar.activation(small[:, 22, :], small[:, 20, :], ACT.Ln, bias=1.0, scale=-1.0).then_inc(ln_out, 1)

            def tT_copies(p):
                for s, bank in ((0, U), (1, V)):
                    act.wait_ge(sv_ready, 7 * p + s + 1)
                    g = pairs[p] + s
                    nc.scalar.copy(outT[:, g * B:(g + 1) * B], bank).then_inc(sv_read, 1)

            def score_copies(p, spare):
                a, b = (slice(g * B, (g + 1) * B) for g in (pairs[p], pairs[p] + 1))
                for n, (to, bank) in enumerate(((left_par_bc[:, a], U), (left_par_bc[:, b], V),
                                                (left_chi_bc[:, a], spare[:, :]), (left_chi_bc[:, b], U))):
                    act.wait_ge(sv_ready, 7 * p + 3 + n)
                    nc.scalar.copy(to, bank).then_inc(sv_read, 1)
                act.wait_ge(sv_ready, 7 * p + 7)
                nc.scalar.copy(right[:, pairs[p] * KT:(pairs[p] + 2) * KT, :],
                               V[:, 0:4 * KT].rearrange("p (k c) -> p k c", c=2)).then_inc(sv_read, 1)

            def acc_copy(pan):
                act.wait_ge(at_used, KT * pan.blocks_end + 5)
                nc.scalar.copy(outT[:, pan.G * B:(pan.G + 1) * B], acc[pan.index % 2][:, :]).then_inc(acc_stored, 1)

            for number, pan in enumerate(panels):
                G, i = pan.G, pan.index
                q, size = i - (NB - 1), NB - G
                tangent_panel = pan.phase == 2 and q >= 3 and q % 2
                if pan.phase == 1 and G >= 2:
                    act.wait_ge(y_done, G - 1)
                before = 0
                for seg in pan.segments:
                    def run(j):
                        prod = 0
                        for n, (b, H0, step, multiplied) in enumerate(seg.items):
                            def high_part(k):
                                h = KT * (seg.blocks + prod) + k + KT * seg.nprod * j
                                act.wait_ge(turned_tile, h + 1)
                                act.wait_ge(at_used, h + 2)
                                nc.scalar.copy(at_hi[:, k, :], TQ[k]).then_inc(hi_done, 1)

                            def row_sum(m):
                                H = H0 + step * j
                                if m == 1:
                                    act.wait_ge(rowsummed_act[b], 2 * seg.a_use[b] + 2 + 2 * j)
                                    act.sem_inc(act_turns, 1)
                                nc.scalar.activation(discard[b], ablk[:, b, m, :], ACT.Copy,
                                                     accum_out=rowparts[:, pan.G % 2, m, bass.ds(H, 1)])\
                                    .then_inc(rowsummed_act[b], 1)

                            if pan.phase == 1:
                                act.wait_ge(a_loaded[b], 16 * (seg.a_use[b] + 1) + 16 * j)
                                act.sem_inc(act_turns, 1)
                            if multiplied:
                                nth = seg.blocks + prod + seg.nprod * j
                                H = H0 + step * j
                                if pan.phase == 1 or q == 0:
                                    act.wait_ge(y_done, H + 1)
                                    act.sem_inc(act_turns, 1)
                                act.wait_ge(at_used, KT * nth + 1)
                                act.sem_inc(act_turns, 1)
                                nc.scalar.copy(y_hi[:, (seg.blocks + prod) % 2, :], y_sb[:, H, :]).then_inc(y_hi_done, 1)
                            for half in range(2):
                                if multiplied:
                                    high_part(2 * half)
                                if pan.phase == 1:
                                    row_sum(half)
                                if multiplied:
                                    high_part(2 * half + 1)
                                if half == 0 and pan.phase == 2 and seg.n == 1:
                                    after_half_block(before + n)
                            prod += multiplied
                            if tangent_panel and seg.n == 1 and before + n == size - 1 == t_after(size):
                                tT_copies((q - 3) // 2)

                    def after_half_block(b):
                        if b == 0 and q >= 3:
                            if q % 2:
                                logarithms((q - 3) // 2)
                            else:
                                score_copies((q - 4) // 2, acc[i % 2])
                        if tangent_panel and b == t_after(size) + 1:
                            tT_copies((q - 3) // 2)

                    each_run(act, seg, run)
                    before += seg.n * len(seg.items)
                    if seg is pan.segments[0] and number and panels[number - 1].phase == 1 and panels[number - 1].multiplies:
                        acc_copy(panels[number - 1])
            score_copies(PAIRS - 2, acc[(i + 1) % 2])
            logarithms(PAIRS - 1)
            tT_copies(PAIRS - 1)
            score_copies(PAIRS - 1, acc[(i + 1) % 2])
            act.drain().then_inc(layer0_over, 1)
            act.wait_ge(layer0_over, 4)

            act.preload_act_table_set("sigmoid_and_others")
            def sigmoids(d, O, C, half, unit):
                act.wait_ge(par_done, unit + 1)
                act.sem_inc(act_turns, 1)
                for k in range(2):
                    c = C * KT + 2 * half + k
                    a = nc.scalar.activation(sig_par[:, d % 3, k, :], left_par_bc[:, bass.ts(O, B)], ACT.Sigmoid,
                                             bias=right[:, c, 0:1])
                a.then_inc(par_sig, 1)
                act.wait_ge(mixed, unit + 1)
                act.sem_inc(act_turns, 1)
                for k in range(2):
                    c = C * KT + 2 * half + k
                    a = nc.scalar.activation(chi[:, d % 5, k, :], left_chi_bc[:, bass.ts(O, B)], ACT.Sigmoid,
                                             bias=right[:, c, 1:2])
                a.then_inc(chi_sig, 1)

            with act.Fori(0, NB) as G:
                for i, r, slot, use, unit in positions(G):
                    H = (G + r) % NB if r else G
                    d = 4 * i
                    if r:
                        for v in range(2):
                            sigmoids(d + v, H, G, v, unit + v)
                        for v in range(2):
                            sigmoids(d + 2 + v, G, H, v, unit + 2 + v)
                    else:
                        for v in range(2):
                            sigmoids(d + v, G, G, v, unit + v)
            for g in range(NB // 2):
                H, d = g + NB // 2, 4 * g
                for v in range(2):
                    sigmoids(d + v, H, g, v, TAIL_UNIT + d + v)
                for v in range(2):
                    sigmoids(d + 2 + v, g, H, v, TAIL_UNIT + d + 2 + v)
            for g in range(NB):
                act.wait_ge(s_turned, g + 1)
                nc.scalar.copy(s_all[:, g, :], T[:, g % 4 // 2, g % 2, :]).then_inc(s_copied, 1)
            act.wait_ge(norm_in, 1)
            nc.scalar.activation(fin[:, 5, :], fin[:, 4, :], ACT.Tanh).then_inc(tanh_out, 1)

        @block.gpsimd
        def _(pool):
            pool.sem_inc(chi_done, 5)
            nc.gpsimd.memset(ident[:, :], 0.0).then_inc(zero_ready, 1)
            pool.wait_ge(zero_ready, 1)
            nc.gpsimd.affine_select(out=ident[:, :], in_=ident[:, :], compare_op=ALU.not_equal, fill=1.0, base=0,
                                    pattern=[[-1, P]], channel_multiplier=1).then_inc(const_ready, 1)
            nc.gpsimd.memset(outT[:, 0:B], 0.0).then_inc(outT_zeroed, 1)

            def centre(g):
                s = g % 2
                pool.wait_ge(mean_ready, g + 1)
                if g >= 2:
                    pool.wait_ge(y_done, g - 1)
                x3 = x_buf[:, s, :].rearrange("p (m d) -> p m d", m=KT)
                c3 = cen_buf[:, s, :].rearrange("p (m d) -> p m d", m=KT)
                nc.gpsimd.tensor_tensor(c3, x3, small[:, s, 0:KT].unsqueeze(2).to_broadcast([P, KT, P]), ALU.subtract)\
                    .then_inc(centred, 1)

            def y_parts(pan, seg, after_block=None):
                def run(j):
                    for n, (_, H0, step, _) in enumerate(seg.prods):
                        ys = (seg.blocks + n) % 2
                        H = H0 + step * j
                        nth = seg.blocks + n + seg.nprod * j
                        pool.wait_ge(y_hi_done, nth + 1)
                        pool.sem_inc(pool_turns, 1)
                        nc.gpsimd.tensor_tensor(y_lo[:, ys, :], y_sb[:, H, :], y_hi[:, ys, :].bitcast(F32), ALU.subtract)\
                            .then_inc(y_split, 1)
                        if after_block:
                            after_block(n)
                if seg.nprod:
                    each_run(pool, seg, run)

            centre(0)
            for pan in pass1:
                G = pan.G
                inside = len(pan.segments) > 1 and pan.segments[-1].n == 1
                for seg in pan.segments:
                    y_parts(pan, seg, (lambda b: centre(G + 1) if b == 0 else None)
                            if seg is pan.segments[-1] and inside and G + 1 < NB else None)
                if G + 1 < NB and not inside:
                    centre(G + 1)

            def pair_rows(v, p):
                return v[pairs[p]:pairs[p] + 2].rearrange("g p m d -> p g m d")

            def buf_rows(buf):
                return buf[:, :, :].rearrange("p g (m d) -> p g m d", m=KT)

            def store_x1(p):
                pool.wait_ge(x1_ready, p + 1)
                pool.dma_start(pair_rows(x1_v, p), buf_rows(x_buf)).then_inc(x1_stored, 16)

            def store_t(p):
                pool.wait_ge(t_ready, p + 1)
                pool.dma_start(pair_rows(t_v, p), buf_rows(t_buf)).then_inc(t_stored, 16)

            def clear(p):
                pool.wait_ge(sv_ready, 7 * p + 7)
                nc.gpsimd.memset(outT[:, pairs[p] * B:(pairs[p] + 2) * B], 0.0).then_inc(outT_zeroed, 1)

            def add_bias(p):
                for s in range(2):
                    pool.wait_ge(x_loaded[s], 16 * (NB // 2 + p + 1))
                    x3 = x_buf[:, s, :].rearrange("p (m d) -> p m d", m=KT)
                    nc.gpsimd.tensor_tensor(x3, x3, b_bc[:, :].unsqueeze(1).to_broadcast([P, KT, P]), ALU.add)\
                        .then_inc(xb_ready, 1)

            for q, pan in enumerate(pass2):
                def after_block(b):
                    if b == 0:
                        add_bias(q // 2 - 1)
                    if b == 1 and q >= 4:
                        clear(q // 2 - 2)

                for n, seg in enumerate(pan.segments):
                    y_parts(pan, seg, after_block if n == 0 and q >= 2 and q % 2 == 0 else None)
                if q >= 2:
                    if q % 2:
                        store_t((q - 3) // 2)
                    else:
                        store_x1(q // 2 - 1)
            add_bias(PAIRS - 1)
            clear(PAIRS - 2)
            store_x1(PAIRS - 1)
            store_t(PAIRS - 1)
            clear(PAIRS - 1)
            pool.wait_ge(x1_stored, 16 * PAIRS)
            pool.wait_ge(t_stored, 16 * PAIRS)
            pool.drain().then_inc(layer0_over, 1)
            pool.wait_ge(layer0_over, 4)

            def times_adj(d, slot, blk, half, unit, use=None):
                if use is not None:
                    pool.wait_ge(pair_loaded[slot], 32 * use + 32)
                pool.wait_ge(chi_sig, unit + 1)
                i = nc.gpsimd.tensor_tensor(chi[:, d % 5, :, :], chi[:, d % 5, :, :],
                                            ablk[:, 2 * slot + blk, 2 * half:2 * half + 2, :], ALU.mult)
                i.then_inc(chi_done, 1)

            with pool.Fori(0, NB) as G:
                for i, r, slot, use, unit in positions(G):
                    if r:
                        for v in range(4):
                            times_adj(4 * i + v, slot, v // 2, v % 2, unit + v, use if v == 0 else None)
                    else:
                        for v in range(2):
                            times_adj(4 * i + v, slot, 1, v, unit + v, use if v == 0 else None)
            for g in range(NB // 2):
                for v in range(4):
                    times_adj(4 * g + v, g % 2, v // 2, v % 2, TAIL_UNIT + 4 * g + v,
                              TAIL_USE + g // 2 if v == 0 else None)
            sq4 = shared[:, 0:N].rearrange("p (g c) -> p g c", c=B)
            pool.wait_ge(outg_added, NB + NB // 2 + 1)
            for g in range(NB):
                if g % 3 != 1:
                    pool.wait_ge(s_copied, g + 1)
                    nc.gpsimd.tensor_tensor(sq4[:, g, :], s_all[:, g, :], s_all[:, g, :], ALU.mult).then_inc(s_squared, 1)
            pool.wait_ge(scale_ready, 1)
            pool.wait_ge(x1_back, 16 * NB)
            for g in range(2, NB, 3):
                s3 = s_all[:, g, :].rearrange("p (m d) -> p m d", m=KT)
                scale = fin[:, 6, g * KT:(g + 1) * KT].unsqueeze(2).to_broadcast([P, KT, P])
                nc.gpsimd.tensor_tensor(s3, s3, scale, ALU.mult).then_inc(s_scaled, 1)
                pool.wait_ge(s_scaled, g // 3 + 1)
                nc.gpsimd.tensor_tensor(s_all[:, g, :], s_all[:, g, :], x1_all[:, g, :], ALU.add).then_inc(fin_ready_pool, 1)

        @block.vector
        def _(dve):
            steps = [0]

            def step(i):
                steps[0] += 1
                i.then_inc(dve_step, 1)
                dve.wait_ge(dve_step, steps[0])

            def rsqrt_seed(r, w, a, sh):
                step(nc.vector.tensor_scalar(a[sh].bitcast(U32), w[sh].bitcast(U32), 1, None, ALU.logical_shift_right))
                step(nc.vector.tensor_scalar(r[sh].bitcast(U32), a[sh].bitcast(U32), -1.0, float(RSQRT_SEED), ALU.mult, ALU.add))

            def newton(r, w, a, sh):
                step(nc.vector.tensor_tensor(a[sh], r[sh], r[sh], ALU.mult))
                step(nc.vector.scalar_tensor_tensor(out=a[sh], in0=a[sh], scalar=-0.5, in1=w[sh], op0=ALU.mult, op1=ALU.mult))
                step(nc.vector.scalar_tensor_tensor(out=r[sh], in0=a[sh], scalar=1.5, in1=r[sh], op0=ALU.add, op1=ALU.mult))

            def rows(a):
                return a.rearrange("p (m d) -> p m d", m=KT)

            def wide(a):
                return a.unsqueeze(2).to_broadcast([P, KT, P])

            for s in range(4):
                dve.sem_inc(rowsummed_dve[s], 1)
            dve.sem_inc(lo_done, 4)
            dve.sem_inc(par_done, 3)
            dve.sem_inc(mixed, 5)
            dve.sem_inc(outh_added, 1)
            dve.sem_inc(outg_added, 1)
            dve.wait_ge(const_loaded, 16 * 8)
            for c in range(2):
                nc.vector.tensor_copy(w_left_rep[:, c, :], w_left[:, c:c + 1].to_broadcast([P, P])).then_inc(reps_ready, 1)

            def mean_of(g):
                s = g % 2
                dve.wait_ge(x_loaded[s], 16 * (g // 2 + 1))
                if g >= 2:
                    dve.wait_ge(centred, g - 1)
                if g:
                    dve.wait_ge(mean_ready, g)
                step(nc.vector.reduce_sum(small[:, 2, 0:KT], rows(x_buf[:, s, :]), AX))
                nc.vector.tensor_scalar(small[:, s, 0:KT], small[:, 2, 0:KT], 1.0 / D, None, ALU.mult).then_inc(mean_ready, 1)

            def low_parts(seg, n, j, half):
                for k in (2 * half, 2 * half + 1):
                    h = KT * (seg.blocks + n) + k + KT * seg.nprod * j
                    dve.wait_ge(hi_done, h + 1)
                    nc.vector.tensor_tensor(at_lo[:, k, :], TQ[k], at_hi[:, k, :].bitcast(F32), ALU.subtract)\
                        .then_inc(lo_done, 1)

            lo, hi = slice(0, KT), slice(KT, 2 * KT)
            both = (slice(None), slice(0, 2 * KT))
            low = (slice(None), lo)
            w1, r1, a1, filled = small[:, 3, :], small[:, 4, :], small[:, 5, :], small[:, 6, :]

            def y_sums(g):
                for s in range(4):
                    dve.wait_ge(rowsummed_dve[s], 4 * (g + 1) + 1)
                    dve.wait_ge(rowsummed_act[s], 8 * (g + 1) + 1)
                step(nc.vector.reduce_sum(w1[:, hi], rowparts[:, g % 2, :, :], AX))
                dve.wait_ge(centred, g + 1)
                step(nc.vector.tensor_tensor(sq_buf[:, g % 2, :], cen_buf[:, g % 2, :], cen_buf[:, g % 2, :], ALU.mult))
                step(nc.vector.reduce_sum(w1[:, lo], rows(sq_buf[:, g % 2, :]), AX))

            def y_variance(g):
                step(nc.vector.tensor_scalar(filled[:, hi], w1[:, hi], 0.0, None, ALU.is_gt))
                step(nc.vector.tensor_scalar(w1[:, lo], w1[:, lo], 1.0 / D, LN_EPS, ALU.mult, ALU.add))
                step(nc.vector.tensor_scalar(w1[:, hi], w1[:, hi], MIN_NORM_SQ, None, ALU.max))

            def y_seed(g):
                rsqrt_seed(r1, w1, a1, both)

            def y_newton(g):
                newton(r1, w1, a1, both)

            def y_scale(g):
                step(nc.vector.tensor_tensor(dinv[:, g * KT:(g + 1) * KT], r1[:, hi], filled[:, hi], ALU.mult))
                step(nc.vector.tensor_tensor(a1[:, lo], r1[:, lo], dinv[:, g * KT:(g + 1) * KT], ALU.mult))

            def y_rows(g):
                nc.vector.scalar_tensor_tensor(out=rows(y_sb[:, g, :]), in0=rows(cen_buf[:, g % 2, :]), scalar=0.0,
                                               in1=wide(a1[:, lo]), op0=ALU.max, op1=ALU.mult).then_inc(y_done, 1)

            Y_STAGES = (y_sums, y_variance, y_seed, y_newton, y_newton, y_newton, y_scale, y_rows)

            mean_of(0)
            for pan in pass1:
                G = pan.G
                staged = 0
                for seg in pan.segments:
                    def run(j, stages=()):
                        prod = 0
                        for n, (b, H0, step_H, multiplied) in enumerate(seg.items):
                            def row_sum(m):
                                H = H0 + step_H * j
                                if m == 2:
                                    dve.wait_ge(a_loaded[b], 16 * (seg.a_use[b] + 1) + 16 * j)
                                i = nc.vector.reduce_sum(rowparts[:, pan.G % 2, m, bass.ds(H, 1)], ablk[:, b, m, :], AX)
                                if m == 3:
                                    i.then_inc(rowsummed_dve[b], 1)

                            for half in range(2):
                                if multiplied:
                                    low_parts(seg, prod, j, half)
                                row_sum(2 + half)
                            prod += multiplied
                            if stages:
                                stages[n](G - 1)

                    if seg is pan.segments[-1] and G and G + 1 < NB and len(pan.segments) > 1:
                        mean_of(G + 1)
                    j = 0
                    while G and staged < len(Y_STAGES) and j < seg.n:
                        run(j, Y_STAGES[staged:staged + 4])
                        staged += 4
                        j += 1
                    if seg.n - j > 1:
                        with dve.Fori(j, seg.n) as jj:
                            run(jj)
                    elif j < seg.n:
                        run(j)
                if G + 1 < NB and (not G or len(pan.segments) == 1):
                    mean_of(G + 1)

            def pair(a):
                return a[:, :, :].rearrange("p s (m d) -> p (s m) d", m=KT)

            def pair_wide(a):
                return a.unsqueeze(2).to_broadcast([P, 2 * KT, P])

            sm, mean, var, w, r, a = (small[:, n, :] for n in (7, 8, 9, 10, 11, 12))
            n2, rn, norm = (small[:, n, :] for n in (13, 14, 15))
            f, x2, poly, near0 = (small[:, n, :] for n in (16, 17, 18, 19))
            al = (slice(None), slice(None))

            def add_passes(q):
                g, i = pass2[q].G, pass2[q].index
                dve.wait_ge(at_used, KT * pass2[q].blocks_end + 5)
                if g:
                    dve.wait_ge(acc_stored, g)
                else:
                    dve.wait_ge(outT_zeroed, 1)
                o = outT[:, g * B:(g + 1) * B]
                nc.vector.tensor_tensor(o, acc[i % 2][:, :], o, ALU.add).then_inc(z_done, 1)

            def scale_rows(p):
                for s, bank in ((0, U), (1, V)):
                    g = pairs[p] + s
                    dve.wait_ge(u_done, 2 * p + s + 1)
                    nc.vector.tensor_tensor(rows(hsq_buf[:, s, :]), rows(bank), wide(dinv[:, g * KT:(g + 1) * KT]), ALU.mult)\
                        .then_inc(u_read, 1)

            def add_x(p):
                dve.wait_ge(u_read, 2 * p + 2)
                dve.wait_ge(xb_ready, 2 * p + 2)
                nc.vector.tensor_tensor(x_buf[:, :, :], hsq_buf[:, :, :], x_buf[:, :, :], ALU.add).then_inc(x1_ready, 1)

            def mean_rows(p):
                dve.wait_ge(x1_ready, p + 1)
                step(nc.vector.reduce_sum(sm, pair(x_buf), AX))
                step(nc.vector.tensor_scalar(mean, sm, 1.0 / D, None, ALU.mult))

            def centre_rows(p):
                nc.vector.tensor_tensor(pair(h_buf), pair(x_buf), pair_wide(mean), ALU.subtract).then_inc(norm_start, 1)
                dve.wait_ge(norm_start, p + 1)

            def square_rows(p):
                step(nc.vector.tensor_tensor(hsq_buf[:, :, :], h_buf[:, :, :], h_buf[:, :, :], ALU.mult))

            def variance(p):
                step(nc.vector.reduce_sum(var, pair(hsq_buf), AX))
                step(nc.vector.tensor_scalar(w, var, 1.0 / D, LN_EPS, ALU.mult, ALU.add))

            def variance_seed(p):
                rsqrt_seed(r, w, a, al)

            def variance_newton(p):
                newton(r, w, a, al)

            def normalise(p):
                step(nc.vector.scalar_tensor_tensor(out=pair(h_buf), in0=pair(h_buf), scalar=0.0, in1=pair_wide(r),
                                                    op0=ALU.max, op1=ALU.mult))

            def norm_squared(p):
                step(nc.vector.reduce_sum(n2, pair(hsq_buf), AX))
                step(nc.vector.tensor_scalar(n2, n2, MIN_NORM_SQ, None, ALU.max))

            def norm_seed(p):
                rsqrt_seed(rn, n2, a, al)

            def norm_newton(p):
                newton(rn, n2, a, al)

            def norm_clipped(p):
                step(nc.vector.tensor_tensor(norm, n2, rn, ALU.mult))
                nc.vector.tensor_scalar(small[:, 20, :], norm, ARTANH_MAX, None, ALU.min).then_inc(ln_in, 1)

            ROW_STAGES = (scale_rows, add_x, mean_rows, centre_rows, square_rows, variance,
                          variance_seed, variance_newton, variance_newton, variance_newton, normalise,
                          square_rows, norm_squared, norm_seed, norm_newton, norm_newton, norm_newton, norm_clipped)

            def half_log_ratio(p):
                dve.wait_ge(ln_out, p + 1)
                step(nc.vector.tensor_tensor(f, small[:, 21, :], small[:, 22, :], ALU.subtract))
                step(nc.vector.scalar_tensor_tensor(out=f, in0=f, scalar=0.5, in1=rn, op0=ALU.mult, op1=ALU.mult))

            def series_start(p):
                step(nc.vector.tensor_scalar(near0, n2, SERIES_SQ, None, ALU.is_lt))
                step(nc.vector.tensor_scalar(x2, n2, SERIES_SQ, None, ALU.min))
                step(nc.vector.tensor_scalar(poly, x2, 1.0 / 13, None, ALU.mult))

            def series(p):
                for o in (11, 9, 7, 5, 3):
                    step(nc.vector.scalar_tensor_tensor(out=poly, in0=poly, scalar=1.0 / o, in1=x2, op0=ALU.add, op1=ALU.mult))

            def series_or_logs(p):
                step(nc.vector.scalar_tensor_tensor(out=poly, in0=poly, scalar=1.0, in1=f, op0=ALU.add, op1=ALU.subtract))
                step(nc.vector.tensor_tensor(poly, poly, near0, ALU.mult))
                step(nc.vector.tensor_tensor(f, f, poly, ALU.add))

            def tangent(p):
                if p:
                    dve.wait_ge(t_stored, 16 * p)
                    dve.wait_ge(sv_ready, 7 * (p - 1) + 2)
                else:
                    for s in range(4):
                        dve.wait_ge(rowsummed_act[s], 8 * NB + 1)
                nc.vector.tensor_tensor(pair(t_buf), pair(h_buf), pair_wide(f), ALU.mult).then_inc(t_ready, 1)
                dve.wait_ge(t_ready, p + 1)

            TANGENT_STAGES = (half_log_ratio, series_start, series, series_or_logs, tangent)

            for q, pan in enumerate(pass2):
                size = NB - pan.G
                if q == 0:
                    stages, of, start, halves = Y_STAGES, NB - 1, 1, 2
                elif q == 1:
                    stages, of, start, halves = (), 0, 0, 1
                elif q % 2 == 0:
                    stages, of, start, halves = ROW_STAGES, q // 2 - 1, 2 * u_after(size) + 3, 2 * size - 1
                else:
                    stages, of, start, halves = TANGENT_STAGES, (q - 3) // 2, 2, 2 * (t_after(size) + 1)
                done = half_blocks = 0
                for seg in pan.segments:
                    for j in range(seg.n):
                        for b in range(seg.nprod):
                            for half in range(2):
                                low_parts(seg, b, j, half)
                                half_blocks += 1
                                if half_blocks == 2 and q:
                                    add_passes(q - 1)
                                if half_blocks >= start and done < len(stages):
                                    due = -(-(len(stages) - done) // (halves - half_blocks + 1))
                                    for stage in stages[done:done + due]:
                                        stage(of)
                                    done += due
            add_passes(NB - 1)
            for stage in ROW_STAGES + TANGENT_STAGES:
                stage(PAIRS - 1)
            dve.wait_ge(sv_read, 7 * PAIRS)
            for c in range(2):
                step(nc.vector.tensor_scalar(right[:, :, c], right[:, :, c], bias2[:, c:c + 1], None, ALU.add))
            dve.wait_ge(outT_zeroed, PAIRS + 1)
            dve.drain().then_inc(layer0_over, 1)
            dve.wait_ge(layer0_over, 4)

            def par(d, unit):
                dve.wait_ge(turned, unit + 6)
                dve.wait_ge(par_sig, unit + 1)
                nc.vector.tensor_tensor(T[:, d % 3, :, :], T[:, d % 3, :, :], sig_par[:, d % 3, :, :], ALU.mult).then_inc(par_done, 1)

            def add_chi(d, unit):
                dve.wait_ge(par_done, unit + 4)
                dve.wait_ge(chi_done, unit + 6)
                dve.wait_ge(unit_used, unit + 4)
                nc.vector.tensor_tensor(mix[:, d % 2, :, :], T[:, d % 3, :, :], chi[:, d % 5, :, :], ALU.add).then_inc(mixed, 1)

            def add_out(block_no, bank, done, used, h_before, g_before):
                dve.wait_ge(unit_used, used + 6)
                dve.wait_ge(outh_added, h_before + 1)
                dve.wait_ge(outg_added, g_before + 1)
                o = outT[:, bass.ts(block_no, B)]
                nc.vector.tensor_tensor(o, bank[:, :], o, ALU.add).then_inc(done, 1)

            outg, outh = acc[0], acc[1]
            par(0, 0)
            for d in range(2):
                add_chi(d, d)
                par(d + 1, d + 1)
            with dve.Fori(0, NB) as G:
                unit0 = UNITS_G * G
                for d in range(2, UNITS_G + 2):
                    add_chi(d % UNITS_G, unit0 + d)
                    if d == UNITS_G + 1:
                        add_out(G, outg, outg_added, unit0 + UNITS_G - 1, 7 * G + 7, G)
                    par((d + 1) % UNITS_G, unit0 + d + 1)
                    if d % 4 == 3 and d < 28:
                        r = d // 4 + 1
                        add_out((G + r) % NB, outh, outh_added, unit0 + d - 2, 7 * G + r - 1, G)
            for d in range(2, 2 * NB):
                g, v = divmod(d, 4)
                add_chi(d, TAIL_UNIT + d)
                if v == 1:
                    add_out(g - 1, outg, outg_added, TAIL_UNIT + d - 2, 7 * NB + g, NB + g - 1)
                if d + 1 < 2 * NB:
                    par(d + 1, TAIL_UNIT + d + 1)
                if v == 3:
                    add_out(g + NB // 2, outh, outh_added, TAIL_UNIT + d - 2, 7 * NB + g, NB + g)
            add_out(NB // 2 - 1, outg, outg_added, TAIL_UNIT + 2 * NB - 1, 7 * NB + NB // 2, NB + NB // 2 - 1)

            sq4 = shared[:, 0:N].rearrange("p (g c) -> p g c", c=B)
            for g in range(NB):
                if g % 3 == 1:
                    dve.wait_ge(s_copied, g + 1)
                    step(nc.vector.tensor_tensor(sq4[:, g, :], s_all[:, g, :], s_all[:, g, :], ALU.mult))
                else:
                    dve.wait_ge(s_squared, g + 1 - (g + 1) // 3)
                step(nc.vector.reduce_sum(fin[:, 0, g * KT:(g + 1) * KT], rows(sq4[:, g, :]), AX))
            al = (slice(None), slice(None))
            step(nc.vector.tensor_scalar(fin[:, 1, :], fin[:, 0, :], MIN_NORM_SQ, None, ALU.max))
            rsqrt_seed(fin[:, 2, :], fin[:, 1, :], fin[:, 3, :], al)
            for _ in range(3):
                newton(fin[:, 2, :], fin[:, 1, :], fin[:, 3, :], al)
            nc.vector.tensor_tensor(fin[:, 4, :], fin[:, 1, :], fin[:, 2, :], ALU.mult).then_inc(norm_in, 1)
            dve.wait_ge(tanh_out, 1)
            nc.vector.scalar_tensor_tensor(out=fin[:, 6, :], in0=fin[:, 5, :], scalar=MAX_NORM, in1=fin[:, 2, :],
                                           op0=ALU.min, op1=ALU.mult).then_inc(scale_ready, 1)
            dve.wait_ge(scale_ready, 1)
            dve.wait_ge(x1_back, 16 * NB)
            for g in range(NB):
                if g % 3 == 2:
                    continue
                for k in range(KT):
                    c = slice(k * P, (k + 1) * P)
                    i = nc.vector.scalar_tensor_tensor(out=s_all[:, g, c], in0=s_all[:, g, c],
                                                       scalar=fin[:, 6, g * KT + k:g * KT + k + 1],
                                                       in1=x1_all[:, g, c], op0=ALU.mult, op1=ALU.add)
                i.then_inc(fin_ready_dve, 1)


_INS = ['x', 'adj', 'L0_gnn_W', 'L0_gnn_b', 'L1_gnn_w_par', 'L1_gnn_b_par', 'L1_gnn_w_chi', 'L1_gnn_b_chi']


def kernel(**inputs):
    import numpy as _np
    import concourse.bacc as _bacc
    from concourse import mybir as _mybir
    from concourse.bass_utils import run_bass_kernel_spmd as _run

    nc = _bacc.Bacc("TRN2", target_bir_lowering=False, num_devices=1)
    arrays, args = {}, []
    for name in _INS:
        a = _np.ascontiguousarray(inputs[name])
        arrays[f"in_{name}"] = a
        args.append(nc.dram_tensor(f"in_{name}", a.shape, _mybir.dt.from_np(a.dtype), kind="ExternalInput").ap())
    shape = arrays["in_x"].shape
    out = nc.dram_tensor("out_dram", shape, _mybir.dt.float32, kind="ExternalOutput").ap()
    x1 = nc.dram_tensor("x1_dram", shape, _mybir.dt.float32, kind="Internal").ap()
    t = nc.dram_tensor("t_dram", shape, _mybir.dt.float32, kind="Internal").ap()
    gnn_kernel(nc, *args, out, x1, t)
    r = _run(nc, [arrays], core_ids=[0])
    return r.results[0]["out_dram"]
```
